# Optimizing a Trainium2 kernel written in Bass

```python
import numpy as np
import jax
import jax.numpy as jnp

def _softmax(x, axis=-1):
    return jax.nn.softmax(x, axis=axis)

def _gelu(x):
    return jax.nn.gelu(x, approximate=True)

def _silu(x):
    return jax.nn.silu(x)

def _sigmoid(x):
    return jax.nn.sigmoid(x)

def _layernorm(x, axis=-1, eps=1e-05):
    m = jnp.mean(x, axis=axis, keepdims=True)
    v = jnp.var(x, axis=axis, keepdims=True)
    return (x - m) / jnp.sqrt(v + eps)

def _scatter_add(tgt, idx, src, axis=0):
    return tgt.at[idx].add(src)

def _segment_sum(src, seg, n):
    return jax.ops.segment_sum(src, seg, n)
kernel_name = 'mk_recurrent_d1_jaxref_r4_9806fb'

def setup_inputs(seed: int=0):
    np.random.seed(seed)
    _w = jnp.asarray

    def _L0_attn_setup():
        import jax, jax.numpy as jnp
        import numpy as np
        B, T, C = (4, 256, 256)
        HS = 64
        H = C // HS

        def wkv7(r, w, k, v, a, b):
            Bn, Tn, Cn = r.shape
            N = Cn // H

            def rs(z):
                return z.reshape(Bn, Tn, H, N).transpose(1, 0, 2, 3)
            r_, w_, k_, v_, a_, b_ = map(rs, (r, w, k, v, a, b))
            decay = jnp.exp(w_)
            S0 = jnp.zeros((Bn, H, N, N), dtype=r.dtype)

            def step(S, inp):
                rt, dt, kt, vt, at, bt = inp
                sa = jnp.einsum('bhij,bhj->bhi', S, at)
                S = S * dt[:, :, None, :] + sa[..., None] * bt[:, :, None, :] + vt[..., None] * kt[:, :, None, :]
                y = jnp.einsum('bhij,bhj->bhi', S, rt)
                return (S, y)
            _, ys = jax.lax.scan(step, S0, (r_, decay, k_, v_, a_, b_))
            return ys.transpose(1, 0, 2, 3).reshape(Bn, Tn, Cn)

        def timemix(x, lambdas, k_A, k_B, g_A, g_B, w_A, w_B, w_miu, a_A, a_B, a_time, x_A, x_B, x_miu, x_time, gn_gamma, gn_beta, rW, kW, vW, oW):
            Bn, Tn, Cn = x.shape
            Hn, Nn = x_time.shape
            x_last = jnp.concatenate([jnp.zeros_like(x[:, :1]), x[:, :-1]], axis=1)
            dx = x_last - x
            xm = x + dx * x_miu
            mix = jnp.tanh(xm @ x_A).reshape(Bn, Tn, 6, 32)
            miu = lambdas + jnp.einsum('btgk,gkc->gbtc', mix, x_B)
            xd = x[None] + dx[None] * miu
            r_in, w_in, k_in, v_in, a_in, g_in = xd
            v = v_in @ vW.T
            r = r_in @ rW.T
            g = jnp.tanh(g_in @ g_A) @ g_B
            w = -jax.nn.softplus(-(w_miu + jnp.tanh(w_in @ w_A) @ w_B)) - 0.5
            k = k_in @ kW.T + jnp.tanh(k_in @ k_A) @ k_B
            k = k / jnp.maximum(jnp.linalg.norm(k, axis=-1, keepdims=True), 1e-12)
            a_gate = jax.nn.sigmoid(a_time + a_in @ a_A @ a_B) * 2.0
            kk = k * jnp.exp(jnp.minimum(w * 0.5, 0.0))
            y = wkv7(r, w, kk, v, -k, k * a_gate)
            eps = 1e-05 * Hn
            yg = y.reshape(Bn * Tn, Hn, Nn)
            mean = yg.mean(-1, keepdims=True)
            var = yg.var(-1, keepdims=True)
            yg = (yg - mean) / jnp.sqrt(var + eps)
            y = yg.reshape(Bn * Tn, Cn) * gn_gamma + gn_beta
            y = y.reshape(Bn, Tn, Cn)
            rh = r.reshape(Bn, Tn, Hn, Nn)
            kh = k.reshape(Bn, Tn, Hn, Nn)
            vh = v.reshape(Bn, Tn, Hn, Nn)
            bonus = ((rh * kh * x_time).sum(-1, keepdims=True) * vh).reshape(Bn, Tn, Cn)
            out = (y + bonus) * g @ oW.T
            return out
        key = jax.random.key(seed)
        ks = jax.random.split(key, 24)
        s = 0.02
        d = {'x': jax.random.normal(ks[0], (B, T, C), jnp.float32), 'lambdas': jax.random.normal(ks[1], (6, 1, 1, C), jnp.float32) * s, 'k_A': jax.random.normal(ks[2], (C, 64), jnp.float32) * s, 'k_B': jax.random.normal(ks[3], (64, C), jnp.float32) * s, 'g_A': jax.random.normal(ks[4], (C, 128), jnp.float32) * s, 'g_B': jax.random.normal(ks[5], (128, C), jnp.float32) * s, 'w_A': jax.random.normal(ks[6], (C, 64), jnp.float32) * s, 'w_B': jax.random.normal(ks[7], (64, C), jnp.float32) * s, 'w_miu': jax.random.normal(ks[8], (1, 1, C), jnp.float32) * s, 'a_A': jax.random.normal(ks[9], (C, 64), jnp.float32) * s, 'a_B': jax.random.normal(ks[10], (64, C), jnp.float32) * s, 'a_time': jax.random.normal(ks[11], (1, 1, C), jnp.float32) * s, 'x_A': jax.random.normal(ks[12], (C, 32 * 6), jnp.float32) * s, 'x_B': jax.random.normal(ks[13], (6, 32, C), jnp.float32) * s, 'x_miu': jax.random.normal(ks[14], (1, 1, C), jnp.float32) * s, 'x_time': jax.random.normal(ks[15], (H, HS), jnp.float32) * s, 'gn_gamma': jnp.ones((C,), jnp.float32), 'gn_beta': jnp.zeros((C,), jnp.float32), 'rW': jax.random.normal(ks[16], (C, C), jnp.float32) * s, 'kW': jax.random.normal(ks[17], (C, C), jnp.float32) * s, 'vW': jax.random.normal(ks[18], (C, C), jnp.float32) * s, 'oW': jax.random.normal(ks[19], (C, C), jnp.float32) * s}
        return d
    _L0_attn_in = _L0_attn_setup()

    def _L0_ffn_setup():
        import jax, jax.numpy as jnp
        import numpy as np
        B, S, D_MODEL, D_FF, E, R, TOP_K = (4, 512, 256, 1024, 8, 16, 2)
        key = jax.random.key(seed)
        ks = jax.random.split(key, 9)
        sd = 1.0 / np.sqrt(D_MODEL)
        return {'hidden_states': jax.random.normal(ks[0], (B, S, D_MODEL), jnp.float32), 'wi': jax.random.normal(ks[1], (D_FF, D_MODEL), jnp.float32) * sd, 'bi': jax.random.normal(ks[2], (D_FF,), jnp.float32) * 0.01, 'wo': jax.random.normal(ks[3], (D_MODEL, D_FF), jnp.float32) * (1.0 / np.sqrt(D_FF)), 'bo': jax.random.normal(ks[4], (D_MODEL,), jnp.float32) * 0.01, 'lora_A': jax.random.normal(ks[5], (E, R, D_MODEL), jnp.float32) * sd, 'lora_B': jax.random.normal(ks[6], (E, D_FF, R), jnp.float32) * 0.02, 'gate_w': jax.random.normal(ks[7], (E, D_MODEL), jnp.float32) * sd, 'gate_b': jax.random.normal(ks[8], (E,), jnp.float32) * 0.01}
    _L0_ffn_in = _L0_ffn_setup()
    _d = {'L0_attn_x': _L0_attn_in['x'], 'L0_attn_lambdas': _L0_attn_in['lambdas'], 'L0_attn_k_A': _L0_attn_in['k_A'], 'L0_attn_k_B': _L0_attn_in['k_B'], 'L0_attn_g_A': _L0_attn_in['g_A'], 'L0_attn_g_B': _L0_attn_in['g_B'], 'L0_attn_w_A': _L0_attn_in['w_A'], 'L0_attn_w_B': _L0_attn_in['w_B'], 'L0_attn_w_miu': _L0_attn_in['w_miu'], 'L0_attn_a_A': _L0_attn_in['a_A'], 'L0_attn_a_B': _L0_attn_in['a_B'], 'L0_attn_a_time': _L0_attn_in['a_time'], 'L0_attn_x_A': _L0_attn_in['x_A'], 'L0_attn_x_B': _L0_attn_in['x_B'], 'L0_attn_x_miu': _L0_attn_in['x_miu'], 'L0_attn_x_time': _L0_attn_in['x_time'], 'L0_attn_gn_gamma': _L0_attn_in['gn_gamma'], 'L0_attn_gn_beta': _L0_attn_in['gn_beta'], 'L0_attn_rW': _L0_attn_in['rW'], 'L0_attn_kW': _L0_attn_in['kW'], 'L0_attn_vW': _L0_attn_in['vW'], 'L0_attn_oW': _L0_attn_in['oW'], 'L0_ffn_wi': _L0_ffn_in['wi'], 'L0_ffn_bi': _L0_ffn_in['bi'], 'L0_ffn_wo': _L0_ffn_in['wo'], 'L0_ffn_bo': _L0_ffn_in['bo'], 'L0_ffn_lora_A': _L0_ffn_in['lora_A'], 'L0_ffn_lora_B': _L0_ffn_in['lora_B'], 'L0_ffn_gate_w': _L0_ffn_in['gate_w'], 'L0_ffn_gate_b': _L0_ffn_in['gate_b']}
    _x0 = _d['L0_attn_x']
    _d['L0_attn_x'] = jax.random.normal(jax.random.fold_in(jax.random.key(seed), 1), (2, 2048, 256), dtype=_x0.dtype)
    del _x0
    return _d

def reference(L0_attn_x, L0_attn_lambdas, L0_attn_k_A, L0_attn_k_B, L0_attn_g_A, L0_attn_g_B, L0_attn_w_A, L0_attn_w_B, L0_attn_w_miu, L0_attn_a_A, L0_attn_a_B, L0_attn_a_time, L0_attn_x_A, L0_attn_x_B, L0_attn_x_miu, L0_attn_x_time, L0_attn_gn_gamma, L0_attn_gn_beta, L0_attn_rW, L0_attn_kW, L0_attn_vW, L0_attn_oW, L0_ffn_wi, L0_ffn_bi, L0_ffn_wo, L0_ffn_bo, L0_ffn_lora_A, L0_ffn_lora_B, L0_ffn_gate_w, L0_ffn_gate_b):

    def _L0_attn_ref(x, lambdas, k_A, k_B, g_A, g_B, w_A, w_B, w_miu, a_A, a_B, a_time, x_A, x_B, x_miu, x_time, gn_gamma, gn_beta, rW, kW, vW, oW):
        import jax, jax.numpy as jnp
        import numpy as np
        B, T, C = (4, 256, 256)
        HS = 64
        H = C // HS

        def wkv7(r, w, k, v, a, b):
            Bn, Tn, Cn = r.shape
            N = Cn // H

            def rs(z):
                return z.reshape(Bn, Tn, H, N).transpose(1, 0, 2, 3)
            r_, w_, k_, v_, a_, b_ = map(rs, (r, w, k, v, a, b))
            decay = jnp.exp(w_)
            S0 = jnp.zeros((Bn, H, N, N), dtype=r.dtype)

            def step(S, inp):
                rt, dt, kt, vt, at, bt = inp
                sa = jnp.einsum('bhij,bhj->bhi', S, at)
                S = S * dt[:, :, None, :] + sa[..., None] * bt[:, :, None, :] + vt[..., None] * kt[:, :, None, :]
                y = jnp.einsum('bhij,bhj->bhi', S, rt)
                return (S, y)
            _, ys = jax.lax.scan(step, S0, (r_, decay, k_, v_, a_, b_))
            return ys.transpose(1, 0, 2, 3).reshape(Bn, Tn, Cn)

        def timemix(x, lambdas, k_A, k_B, g_A, g_B, w_A, w_B, w_miu, a_A, a_B, a_time, x_A, x_B, x_miu, x_time, gn_gamma, gn_beta, rW, kW, vW, oW):
            Bn, Tn, Cn = x.shape
            Hn, Nn = x_time.shape
            x_last = jnp.concatenate([jnp.zeros_like(x[:, :1]), x[:, :-1]], axis=1)
            dx = x_last - x
            xm = x + dx * x_miu
            mix = jnp.tanh(xm @ x_A).reshape(Bn, Tn, 6, 32)
            miu = lambdas + jnp.einsum('btgk,gkc->gbtc', mix, x_B)
            xd = x[None] + dx[None] * miu
            r_in, w_in, k_in, v_in, a_in, g_in = xd
            v = v_in @ vW.T
            r = r_in @ rW.T
            g = jnp.tanh(g_in @ g_A) @ g_B
            w = -jax.nn.softplus(-(w_miu + jnp.tanh(w_in @ w_A) @ w_B)) - 0.5
            k = k_in @ kW.T + jnp.tanh(k_in @ k_A) @ k_B
            k = k / jnp.maximum(jnp.linalg.norm(k, axis=-1, keepdims=True), 1e-12)
            a_gate = jax.nn.sigmoid(a_time + a_in @ a_A @ a_B) * 2.0
            kk = k * jnp.exp(jnp.minimum(w * 0.5, 0.0))
            y = wkv7(r, w, kk, v, -k, k * a_gate)
            eps = 1e-05 * Hn
            yg = y.reshape(Bn * Tn, Hn, Nn)
            mean = yg.mean(-1, keepdims=True)
            var = yg.var(-1, keepdims=True)
            yg = (yg - mean) / jnp.sqrt(var + eps)
            y = yg.reshape(Bn * Tn, Cn) * gn_gamma + gn_beta
            y = y.reshape(Bn, Tn, Cn)
            rh = r.reshape(Bn, Tn, Hn, Nn)
            kh = k.reshape(Bn, Tn, Hn, Nn)
            vh = v.reshape(Bn, Tn, Hn, Nn)
            bonus = ((rh * kh * x_time).sum(-1, keepdims=True) * vh).reshape(Bn, Tn, Cn)
            out = (y + bonus) * g @ oW.T
            return out
        return timemix(x, lambdas, k_A, k_B, g_A, g_B, w_A, w_B, w_miu, a_A, a_B, a_time, x_A, x_B, x_miu, x_time, gn_gamma, gn_beta, rW, kW, vW, oW)

    def _L0_ffn_ref(hidden_states, wi, bi, wo, bo, lora_A, lora_B, gate_w, gate_b):
        import jax, jax.numpy as jnp
        import numpy as np
        B, S, D_MODEL, D_FF, E, R, TOP_K = (4, 512, 256, 1024, 8, 16, 2)
        logits = jnp.einsum('bsd,ed->bse', hidden_states, gate_w) + gate_b
        scores = jax.nn.softmax(logits, axis=-1)
        top_v, top_i = jax.lax.top_k(scores, TOP_K)
        val_sum = top_v.sum(axis=-1)
        out = jnp.zeros_like(hidden_states)
        for e in range(E):
            count = (top_i == e).sum(axis=-1).astype(hidden_states.dtype)
            gate = count * val_sum
            inter = jnp.einsum('bsd,fd->bsf', hidden_states, wi) + bi + jnp.einsum('bsr,fr->bsf', jnp.einsum('bsd,rd->bsr', hidden_states, lora_A[e]), lora_B[e])
            h = jax.nn.relu(inter)
            expert_out = jnp.einsum('bsf,df->bsd', h, wo) + bo
            out = out + gate[..., None] * expert_out
        return out
    x = L0_attn_x
    xn = _layernorm(x, axis=-1)
    s = _L0_attn_ref(xn, L0_attn_lambdas, L0_attn_k_A, L0_attn_k_B, L0_attn_g_A, L0_attn_g_B, L0_attn_w_A, L0_attn_w_B, L0_attn_w_miu, L0_attn_a_A, L0_attn_a_B, L0_attn_a_time, L0_attn_x_A, L0_attn_x_B, L0_attn_x_miu, L0_attn_x_time, L0_attn_gn_gamma, L0_attn_gn_beta, L0_attn_rW, L0_attn_kW, L0_attn_vW, L0_attn_oW)
    g = _silu(_L0_ffn_ref(xn, L0_ffn_wi, L0_ffn_bi, L0_ffn_wo, L0_ffn_bo, L0_ffn_lora_A, L0_ffn_lora_B, L0_ffn_gate_w, L0_ffn_gate_b))
    x = x + s * g
    return x

_drawn_inputs = setup_inputs


def setup_inputs(seed=0):
    import zlib

    import numpy as np

    out = dict(_drawn_inputs(seed))
    spreads = {'L0_attn_gn_gamma': (1.0, 0.6), 'L0_attn_gn_beta': (0.0, 0.8)}
    factors = {'L0_attn_lambdas': 8.0,
     'L0_attn_k_A': 8.0,
     'L0_attn_k_B': 8.0,
     'L0_attn_g_A': 5.288,
     'L0_attn_g_B': 5.299,
     'L0_attn_w_A': 8.0,
     'L0_attn_w_B': 8.0,
     'L0_attn_w_miu': 8.0,
     'L0_attn_a_A': 8.0,
     'L0_attn_a_B': 8.0,
     'L0_attn_a_time': 198.383,
     'L0_attn_x_A': 8.0,
     'L0_attn_x_B': 8.0,
     'L0_attn_x_miu': 8.0,
     'L0_attn_x_time': 8.0,
     'L0_attn_rW': 5.334,
     'L0_attn_kW': 5.31,
     'L0_attn_vW': 5.324,
     'L0_attn_oW': 5.285,
     'L0_ffn_wi': 6.925,
     'L0_ffn_bi': 52.337,
     'L0_ffn_wo': 5.676,
     'L0_ffn_bo': 200.0,
     'L0_ffn_lora_A': 8.0,
     'L0_ffn_lora_B': 8.0,
     'L0_ffn_gate_w': 8.0,
     'L0_ffn_gate_b': 8.0}
    for name, (base, spread) in spreads.items():
        noise = np.random.default_rng([zlib.crc32(name.encode()), seed]).standard_normal(out[name].shape)
        drawn = base * np.exp(spread * noise) if base else spread * noise
        out[name] = jnp.asarray(drawn.astype(out[name].dtype))
    for name, factor in factors.items():
        out[name] = (out[name] * factor).astype(out[name].dtype)
    return out
```

```python
import concourse.bass as bass
from concourse import mybir
from contextlib import ExitStack
import math

F32 = mybir.dt.float32
I32 = mybir.dt.int32
ALU = mybir.AluOpType
ACT = mybir.ActivationFunctionType
AX = mybir.AxisListType

B, T, C = 2, 2048, 256
H, N = 4, 64
L = 128
TILES = T // L
E, RANK, FF = 8, 16, 1024
LEVELS = int(math.log2(L))
HALF = L // 2
EPS_LN, EPS_GN = 1e-5, 1e-5 * H
R_, W_, K_, V_, A_, G_ = range(6)
MIX_ORDER = [W_, K_, A_, R_, V_, G_]
SLOT = {q: k for k, q in enumerate(MIX_ORDER)}
PAIRS = FF // 256
P_LAM, P_WMIU, P_ATIME, P_XMIU, P_XTIME, P_BI, P_COLS = 0, 12, 14, 16, 18, 20, 28


def program(nc, x, par, weights, consts, out):
    ctx = ExitStack()
    with ctx:
        def sb(name, shape, dt=F32):
            return ctx.enter_context(nc.sbuf_tensor(name, shape, dt))

        sems = {}

        def S(name):
            if name not in sems:
                sems[name] = ctx.enter_context(nc.semaphore(name))
            return sems[name]

        go = ctx.enter_context(nc.semaphore("tile_go"))
        loaded = ctx.enter_context(nc.semaphore("weights_loaded"))
        zeroed = ctx.enter_context(nc.semaphore("buffers_zeroed"))

        w = {k: sb("w_" + k, list(v.shape)) for k, v in weights.items()}
        cst = {k: sb("c_" + k, list(v.shape), v.dtype) for k, v in consts.items()}
        prm = sb("prm", [128, P_COLS])
        ident, ones, headsel = cst["ident"], cst["ones"], cst["headsel"]
        mask_g, mask_x, mask_d, rev8 = cst["mask_g"], cst["mask_x"], cst["mask_d"], cst["rev8"]

        x_in = sb("x_in", [128, B, C])
        x_res = sb("x_res", [128, B, C])
        st6 = sb("st6", [128, B, 6])
        mv = sb("mv", [128, B, 2])
        rstd = sb("rstd", [128, B])
        eps = sb("eps", [128, 2])
        xn = sb("xn", [128, B, C])
        xnc = sb("xnc", [128, 2, B, L + 1])
        dx = sb("dx", [128, 2, B * L])
        xm = sb("xm", [128, 2, B * L])
        mixt = sb("mixt", [128, 2, B * L])
        mtmp = sb("mtmp", [128, 2, 2, B * L])
        xd = sb("xd", [128, 6, 2, B * L])
        lg = sb("lg", [128, B, E])
        top8 = sb("top8", [128, B, 8])
        nm1 = sb("nm1", [128, B])
        e8 = sb("e8", [128, B, E])
        esum = sb("esum", [128, B])
        e2 = sb("e2", [128, B])
        vsum = sb("vsum", [128, B])
        hit = sb("hit", [128, B, E])
        hmx = sb("hmx", [128, B])
        oh1 = sb("oh1", [128, B, E])
        oh2 = sb("oh2", [128, B, E])
        rest = sb("rest", [128, B, E])
        xmask = sb("xmask", [128, 2, B, 128])
        xmt = sb("xmt", [128, 2, B * L])
        relu1 = sb("relu1", [128, 2, 512])
        relu2 = sb("relu2", [128, 2, 512])
        hid = sb("hid", [128, 2, 512])
        y1 = sb("y1", [128, B, C])
        ysg = sb("ysg", [128, B, C])
        fgate = sb("fgate", [128, B, C])
        h_w = sb("h_w", [64, B * L])
        h_k = sb("h_k", [64, B * L])
        h_a = sb("h_a", [64, B * L])
        h_g = sb("h_g", [128, B * L])
        sig = sb("sig", [128, B, 2, L])
        rootd = sb("rootd", [128, B, 2, L])
        agate = sb("agate", [128, B, 2, L])
        kraw = sb("kraw", [128, B, 2, L])
        ksq = sb("ksq", [128, 2, B * L])
        nrm = sb("nrm", [128, B, L])
        nrm1 = sb("nrm1", [128, B, L])
        kinv = sb("kinv", [128, B, L])
        rr = sb("rr", [128, B, 2, L])
        kh = sb("kh", [128, B, 2, L])
        vt = sb("vt", [128, B, C])
        gate = sb("gate", [128, B, C])
        dg = sb("dg", [128, 3, B, 2, L])
        bonus = sb("bonus", [128, B, H])
        ar = sb("ar", [128, B, 2, 2, L])
        bk = sb("bk", [128, B, 2, 2, L])
        tot = [sb(f"tot{l}", [128, B, 2, L >> l]) for l in range(LEVELS + 1)]
        gm = sb("gm", [128, B, 2, 2, 2, 2, L])
        tinv = sb("tinv", [128, B, H, L])
        tinvT = sb("tinvT", [128, B, H, L])
        xb = sb("xb", [128, B, H, HALF])
        pp = sb("pp", [128, B, H, N])
        sa = sb("sa", [128, B, H, N])
        bkt = sb("bkt", [128, B, 2, 2, L])
        state = sb("state", [128, B, 2, 2 * N])
        yy = sb("yy", [128, B, H, N])
        s8 = sb("s8", [128, B * H])
        mean8 = sb("mean8", [128, B * H])
        yc = sb("yc", [128, B * H, N])
        ysq = sb("ysq", [128, B * H, N])
        v8 = sb("v8", [128, B * H])
        sd8 = sb("sd8", [128, B * H])
        rs8 = sb("rs8", [128, B * H])
        yn = sb("yn", [128, B, C])
        yn2 = sb("yn2", [128, B, C])
        bv = sb("bv", [128, B, H, N])
        zz = sb("zz", [128, B, C])
        zt = sb("zt", [128, 2, B, L])
        of = sb("of", [128, B, C])
        out_t = sb("out_t", [128, B, C])
        scratch = sb("scratch", [128, 4])
        scratchp = sb("scratchp", [128, 4])

        bank = [ctx.enter_context(nc.psum_tensor(f"bank{i}", [128, 512], F32)) for i in range(8)]
        GB, CB, ZB = [bank[0], bank[1]], [bank[2], bank[3]], [bank[5], bank[6]]
        DB, FB = bank[4], bank[7]

        NW = len(weights) + len(consts) + 1
        NZ = 6
        block = ctx.enter_context(nc.Block())

        def slot(h):
            return 2 * (h % 2) + h // 2

        def left(v, m):
            return v.rearrange("p (n two m) -> p n two m", two=2, m=m)[:, :, 0, :]

        def gct(psum):
            return psum.rearrange("p (c g t) -> p g c t", c=2, g=B)

        PIECES = [[("diff", 0), ("diff", 1)], [("base", 2), ("lora", 2)], [("down", 0)], [("base", 3), ("lora", 3)],
                  [("down", 1), ("diff", 2)], [("diff", 3), ("down", 2)], [("down", 3)]]

        @block.tensor
        def _(pe):
            mm = nc.tensor.matmul
            tr = nc.tensor.transpose

            def ffn(kind, p):
                z, q = ZB[p % 2], p % 2
                if kind == "base":
                    if p >= 2:
                        pe.wait_ge(S("relu2_done"), 2 * (p - 2) + 2)
                    for j in range(2):
                        for c in range(2):
                            f = (2 * p + j) * 128
                            mm(z[:, j * 256:(j + 1) * 256], w["wi"][:, c, f:f + 128], xnc[:, c, :, 1:L + 1],
                               start=(j == 0 and c == 0), stop=False, skip_group_check=True)
                if kind in ("lora", "diff"):
                    e = 0 if kind == "lora" else 1
                    if kind == "lora":
                        pe.wait_ge(S("xmt_done"), 1)
                    else:
                        pe.wait_ge(S("relu1_done"), 2 * p + 2)
                    for j in range(2):
                        f = (2 * p + j) * 128
                        last = mm(z[:, j * 256:(j + 1) * 256], w["lora_B"][:, f:f + 128], xmt[:, e, :],
                                  start=False, stop=True, skip_group_check=True)
                    last.then_inc(S("z1_mm" if kind == "lora" else "z2_mm"), 1)
                if kind == "down":
                    pe.wait_ge(S("hid_done"), p + 1)
                    for j in range(2):
                        for g in range(B):
                            f = 2 * p + j
                            last = mm(FB[:, g * C:(g + 1) * C], hid[:, q, j * 256 + g * L:j * 256 + (g + 1) * L],
                                      w["wo"][:, f, :], start=(f == 0 and g == 0), stop=(f == 2 * PAIRS - 1),
                                      skip_group_check=True)
                    last.then_inc(S("down_mm"), 1)

            def mixed(k):
                q = MIX_ORDER[k]
                o, u = 32 * (q % 4), q // 4
                if k == 0:
                    pe.wait_ge(S("mixt_done"), 2)
                if k >= 3:
                    pe.wait_ge(S("miu_read"), 2 * (k - 3) + 2)
                for c in range(2):
                    last = mm(bank[2 + k % 3][:, c * 256:(c + 1) * 256], w["x_B"][o:o + 32, u, c * 128:(c + 1) * 128],
                              mixt[o:o + 32, u, :], start=True, stop=True)
                last.then_inc(S("miu_mm"), 1)

            def low(dst, name, q, m):
                for c in range(2):
                    last = mm(dst[0:m, 0:B * L], w[name][:, c, :], xd[:, q, c, :], start=(c == 0), stop=(c == 1))
                last.then_inc(S(name + "_mm"), 1)

            def gram(l, g, p):
                n, m = 2 * l + g, 1 << l
                if l == 0:
                    if p == 0 and g == 0:
                        pe.wait_ge(S("ar_ready"), 2)
                        pe.wait_ge(S("bk_ready"), 2)
                        pe.wait_ge(S("v_done"), 1)
                        pe.wait_ge(S("gate_done"), 1)
                else:
                    pe.wait_ge(S("ar_scaled"), 2 * (l - 1) + g + 1)
                    pe.wait_ge(S("bk_scaled"), 2 * (l - 1) + g + 1)
                if n:
                    pe.wait_ge(S(f"g{p}_stored"), n)
                o = 64 * p
                for kind in range(2):
                    for c in range(2):
                        rhs = ar[o:o + 64, g, :, c, :].rearrange("p a (n two m) -> p a n two m", two=2, m=m)[:, :, :, 1, :]
                        last = mm(GB[p][:, (2 * kind + c) * 128:(2 * kind + c + 1) * 128], bk[o:o + 64, g, kind, c, :], rhs,
                                  start=True, stop=True)
                last.then_inc(S(f"g{p}_mm"), 1)

            def inv_x(l, g):
                m = 1 << l
                pe.wait_ge(S("tr_done"), 2 * (l - 1) + g + 1)
                pe.wait_ge(S("g0_stored"), 2 * l + g + 1)
                pe.wait_ge(S("g1_stored"), 2 * l + g + 1)
                for h in range(H):
                    last = mm(CB[g][:, h * HALF:(h + 1) * HALF], gm[:, g, h // 2, 0, h % 2, 0, :], left(tinv[:, g, h, :], m),
                              start=True, stop=True)
                last.then_inc(S("x_mm"), 1)

            def inv_off(l, g):
                pe.wait_ge(S("x_done"), 2 * (l - 1) + g + 1)
                for h in range(H):
                    last = mm(CB[g][:, 256 + h * HALF:256 + (h + 1) * HALF], tinvT[:, g, h, :], xb[:, g, h, :],
                              start=True, stop=True)
                last.then_inc(S("off_mm"), 1)

            def inv_tr(l, g):
                if l == 0:
                    pe.wait_ge(S("inv1_done"), 2 * g + 2)
                    pe.wait_ge(S("hg_done" if g == 0 else "ksq_done"), 1)
                else:
                    pe.wait_ge(S("inv_added"), 2 * (l - 1) + g + 1)
                for h in range(H):
                    last = tr(CB[g][:, h * L:(h + 1) * L], (tinvT if l == 0 else tinv)[:, g, h, :], ident[:])
                last.then_inc(S("tr_mm"), 1)

            pe.wait_ge(loaded, 16 * NW)
            pe.wait_ge(zeroed, NZ)
            with pe.Fori(0, TILES) as i:
                pe.wait_ge(go, i + 1)
                mm(DB[:, 0:128], ident[:], ident[:], start=True, stop=True)
                pe.wait_ge(S("xn_done"), B)
                for c in range(2):
                    for g in range(B):
                        last = tr(bank[0][:, (c * B + g) * L:(c * B + g + 1) * L], xn[:, g, c * 128:(c + 1) * 128], ident[:])
                last.then_inc(S("xt_mm"), 1)
                pe.wait_ge(S("xnc_done"), 1)
                for g in range(B):
                    for c in range(2):
                        last = mm(bank[1][:, g * 136:(g + 1) * 136], xnc[:, c, g, 1:L + 1], w["route"][:, c, :],
                                  start=(c == 0), stop=(c == 1))
                last.then_inc(S("route_mm"), 1)
                ffn("base", 0)
                pe.wait_ge(S("xm_done"), 2)
                for u, m in ((0, 128), (1, 64)):
                    for c in range(2):
                        last = mm(bank[0][0:m, u * 256:(u + 1) * 256], w["x_A"][:, c, u * 128:u * 128 + m], xm[:, c, :],
                                  start=(c == 0), stop=(c == 1))
                last.then_inc(S("mix_mm"), 1)
                ffn("base", 1)
                pe.wait_ge(S("xmask_done"), 2)
                for j in range(2):
                    for g in range(B):
                        last = tr(bank[1][:, (j * B + g) * L:(j * B + g + 1) * L], xmask[:, j, g, :], ident[:])
                last.then_inc(S("xmt_mm"), 1)
                mixed(0)
                mixed(1)
                mixed(2)
                ffn("lora", 0)
                pe.wait_ge(S("xd_done"), SLOT[W_] + 1)
                low(bank[0], "w_A", W_, 64)
                mixed(3)
                pe.wait_ge(S("xd_done"), SLOT[K_] + 1)
                low(bank[1], "k_A", K_, 64)
                pe.wait_ge(S("xd_done"), SLOT[A_] + 1)
                pe.wait_ge(S("hw_done"), 1)
                low(bank[0], "a_A", A_, 64)
                mixed(4)
                pe.wait_ge(S("miu_read"), 8)
                for c in range(2):
                    last = mm(bank[2][:, c * 256:(c + 1) * 256], w["w_B"][0:64, c * 128:(c + 1) * 128], h_w[:],
                              start=True, stop=True)
                last.then_inc(S("w_B_mm"), 1)
                pe.wait_ge(S("miu_read"), 10)
                for c in range(2):
                    for k in range(2):
                        mm(bank[3][:, c * 256:(c + 1) * 256], w["kW"][:, k, c * 128:(c + 1) * 128], xd[:, K_, k, :],
                           start=(c == 0 and k == 0), stop=False, skip_group_check=True)
                mixed(5)
                ffn("lora", 1)
                pe.wait_ge(S("xd_done"), SLOT[R_] + 1)
                pe.wait_ge(S("miu_read"), 12)
                for c in range(2):
                    for k in range(2):
                        last = mm(bank[4][:, c * 256:(c + 1) * 256], w["rW"][:, k, c * 128:(c + 1) * 128], xd[:, R_, k, :],
                                  start=(k == 0), stop=(k == 1))
                last.then_inc(S("r_mm"), 1)
                pe.wait_ge(S("ha_done"), 1)
                pe.wait_ge(S("hk_done"), 1)
                for c in range(2):
                    last = mm(bank[1][:, c * 256:(c + 1) * 256], w["a_B"][0:64, c * 128:(c + 1) * 128], h_a[:],
                              start=True, stop=True)
                last.then_inc(S("a_B_mm"), 1)
                for c in range(2):
                    last = mm(bank[3][:, c * 256:(c + 1) * 256], w["k_B"][0:64, c * 128:(c + 1) * 128], h_k[:],
                              start=False, stop=True, skip_group_check=True)
                last.then_inc(S("k_mm"), 1)
                pe.wait_ge(S("xd_done"), SLOT[V_] + 1)
                for g in range(B):
                    for k in range(2):
                        last = mm(bank[0][:, g * C:(g + 1) * C], xd[:, V_, k, g * L:(g + 1) * L], w["vW"][:, k, :],
                                  start=(k == 0), stop=(k == 1))
                last.then_inc(S("v_mm"), 1)
                pe.wait_ge(S("xd_done"), SLOT[G_] + 1)
                pe.wait_ge(S("sig_done"), 2)
                low(bank[2], "g_A", G_, 128)
                pe.wait_ge(S("ksq_done"), 1)
                pe.wait_ge(S("r_done"), 1)
                for c in range(2):
                    last = mm(DB[:, 0:B * L], ones[:], ksq[:, c, :], start=(c == 0), stop=(c == 1))
                last.then_inc(S("nrm_mm"), 1)
                pe.wait_ge(S("hg_done"), 1)
                pe.wait_ge(S("agate_done"), 2)
                for g in range(B):
                    last = mm(bank[1][:, g * C:(g + 1) * C], h_g[:, g * L:(g + 1) * L], w["g_B"][:], start=True, stop=True)
                last.then_inc(S("gate_mm"), 1)
                pe.wait_ge(S("dg_done"), 2)
                pe.wait_ge(S("dg2_done"), 2)
                pe.wait_ge(S("nrm_done"), 1)
                for g in range(B):
                    for j in range(3):
                        for c in range(2):
                            o = (g * 3 + j) * H + c
                            last = mm(DB[:, o:o + 3:2], dg[:, j, g, c, :], headsel[:], start=True, stop=True)
                last.then_inc(S("diag_mm"), 1)
                for l in range(LEVELS):
                    if l >= 2:
                        inv_x(l - 1, 0)
                        inv_x(l - 1, 1)
                    gram(l, 0, 0)
                    gram(l, 0, 1)
                    if l >= 2:
                        inv_off(l - 1, 0)
                    gram(l, 1, 0)
                    if l >= 2:
                        inv_off(l - 1, 1)
                    gram(l, 1, 1)
                    ffn(*PIECES[l][0])
                    if l >= 1:
                        inv_tr(l - 1, 0)
                    for piece in PIECES[l][1:]:
                        ffn(*piece)
                    if l >= 1:
                        inv_tr(l - 1, 1)
                top = LEVELS - 1
                inv_x(top, 0)
                inv_x(top, 1)
                for g in range(B):
                    pe.wait_ge(S("ar_scaled"), 2 * top + g + 1)
                    pe.wait_ge(S("g0_stored"), 2 * LEVELS)
                    pe.wait_ge(S("g1_stored"), 2 * LEVELS)
                    for c in range(2):
                        mm(GB[g][:, c * 128:(c + 1) * 128], ar[:, g, 0, c, :], state[:, g, c, :], start=True, stop=False,
                           skip_group_check=True)
                        for h in (2 * c, 2 * c + 1):
                            last = mm(GB[g][:, h * N:(h + 1) * N], gm[:, g, h % 2, 1, c, 0, :], vt[:, g, h * N:(h + 1) * N],
                                      start=False, stop=True, skip_group_check=True)
                    last.then_inc(S("p_mm"), 1)
                inv_off(top, 0)
                inv_off(top, 1)
                for g in range(B):
                    pe.wait_ge(S("bk_scaled"), 2 * top + g + 1)
                    pe.wait_ge(S("diag_read"), 5)
                    if g:
                        pe.wait_ge(S("bkt_done"), g)
                    for j in range(2):
                        for c in range(2):
                            last = tr(DB[:, (j * 2 + c) * L:(j * 2 + c + 1) * L], bk[:, g, j, c, :], ident[:])
                    last.then_inc(S("bkt_mm"), 1)
                inv_tr(top, 0)
                inv_tr(top, 1)
                for g in range(B):
                    pe.wait_ge(S("tr_done"), 2 * top + g + 1)
                    pe.wait_ge(S("p_done"), g + 1)
                    for h in range(H):
                        last = mm(GB[g][:, 256 + h * N:256 + (h + 1) * N], tinvT[:, g, slot(h), :], pp[:, g, h, :],
                                  start=True, stop=True)
                    last.then_inc(S("sa_mm"), 1)
                for g in range(B):
                    pe.wait_ge(S("sa_done"), g + 1)
                    pe.wait_ge(S("diag_read"), 5)
                    for c in range(2):
                        mm(CB[g][:, c * 128:(c + 1) * 128], ar[:, g, 1, c, :], state[:, g, c, :], start=True, stop=False,
                           skip_group_check=True)
                        for h in (2 * c, 2 * c + 1):
                            dst = CB[g][:, h * N:(h + 1) * N]
                            mm(dst, gm[:, g, h % 2, 0, c, 1, :], sa[:, g, h, :], start=False, stop=False,
                               skip_group_check=True)
                            last = mm(dst, gm[:, g, h % 2, 1, c, 1, :], vt[:, g, h * N:(h + 1) * N], start=False, stop=True,
                                      skip_group_check=True)
                    last.then_inc(S("y_mm"), 1)
                    pe.wait_ge(S("bkt_done"), g + 1)
                    for c in range(2):
                        dst = GB[g][:, c * 128:(c + 1) * 128]
                        mm(dst, bkt[:, g, 0, c, :], sa[:, g, 2 * c:2 * c + 2, :], start=True, stop=False)
                        last = mm(dst, bkt[:, g, 1, c, :], vt[:, g, c * 128:(c + 1) * 128], start=False, stop=True)
                    last.then_inc(S("inc_mm"), 1)
                pe.wait_ge(S("zz_done"), 1)
                for c in range(2):
                    for g in range(B):
                        last = tr(DB[:, (c * B + g) * L:(c * B + g + 1) * L], zz[:, g, c * 128:(c + 1) * 128], ident[:])
                last.then_inc(S("zt_mm"), 1)
                pe.wait_ge(S("zt_done"), 1)
                for g in range(B):
                    for c in range(2):
                        last = mm(CB[0][:, g * C:(g + 1) * C], zt[:, c, g, :], w["oW"][:, c, :], start=(c == 0), stop=(c == 1))
                last.then_inc(S("o_mm"), 1)

        @block.scalar
        def _(act):
            A = nc.scalar.activation

            def relu(which, p):
                act.wait_ge(S(f"z{which}_mm"), p + 1)
                if p >= 2:
                    act.wait_ge(S("hid_done"), p - 1)
                dst = relu1 if which == 1 else relu2
                for j in range(2):
                    A(dst[:, p % 2, j * 256:(j + 1) * 256], ZB[p % 2][:, j * 256:(j + 1) * 256], ACT.Relu,
                      bias=prm[:, P_BI + 2 * p + j:P_BI + 2 * p + j + 1]).then_inc(S(f"relu{which}_done"), 1)

            def inv_tr(l, g):
                act.wait_ge(S("tr_mm"), 2 * l + g + 1)
                dst = tinv if l == 0 else tinvT
                A(dst[:, g, :, :], CB[g][:, :], ACT.Copy).then_inc(S("tr_done"), 1)

            act.wait_ge(loaded, 16 * NW)
            act.wait_ge(zeroed, NZ)
            with act.Fori(0, TILES) as i:
                act.wait_ge(go, i + 1)
                A(scratch[:, 0:1], eps[:, 0:1], ACT.Copy)
                act.wait_ge(S("var_done"), B)
                A(rstd[:, :], mv[:, :, 1], ACT.Sqrt, bias=eps[:, 0:1]).then_inc(S("std_done"), 1)
                A(x_res[:, :, :], x_in[:, :, :], ACT.Copy).then_inc(S("xres_done"), 1)
                act.wait_ge(S("xt_mm"), 1)
                act.wait_ge(S("carry_done"), 1)
                A(xnc[:, :, :, 1:L + 1], bank[0][:, :].rearrange("p (c g t) -> p c g t", c=2, g=B), ACT.Copy)\
                    .then_inc(S("xnc_done"), 1)
                act.wait_ge(S("mix_mm"), 1)
                A(mixt[:, 0, :], bank[0][:, 0:256], ACT.Tanh).then_inc(S("mixt_done"), 1)
                A(mixt[0:64, 1, :], bank[0][0:64, 256:512], ACT.Tanh).then_inc(S("mixt_done"), 1)
                act.wait_ge(S("xmt_mm"), 1)
                A(xmt[:, :, :], bank[1][:, :], ACT.Copy).then_inc(S("xmt_done"), 1)
                for g in range(B):
                    A(tinvT[:, g, :, :], ident[:].unsqueeze(1).to_broadcast([128, H, L]), ACT.Copy)\
                        .then_inc(S("inv0_done"), 1)
                relu(1, 0)
                act.wait_ge(S("w_A_mm"), 1)
                A(h_w[:], bank[0][0:64, 0:256], ACT.Tanh).then_inc(S("hw_done"), 1)
                act.wait_ge(S("k_A_mm"), 1)
                A(h_k[:], bank[1][0:64, 0:256], ACT.Tanh).then_inc(S("hk_done"), 1)
                act.wait_ge(S("a_A_mm"), 1)
                A(h_a[:], bank[0][0:64, 0:256], ACT.Copy).then_inc(S("ha_done"), 1)
                act.wait_ge(S("w_B_mm"), 1)
                for c in range(2):
                    A(sig[:, :, c, :], bank[2][:, c * 256:(c + 1) * 256].rearrange("p (g t) -> p g t", g=B), ACT.Sigmoid,
                      bias=prm[:, P_WMIU + c:P_WMIU + c + 1]).then_inc(S("sig_done"), 1)
                relu(1, 1)
                act.wait_ge(S("r_mm"), 1)
                A(rr[:, :, :, :], gct(bank[4][:, :]), ACT.Copy).then_inc(S("r_done"), 1)
                act.wait_ge(S("a_B_mm"), 1)
                for c in range(2):
                    A(agate[:, :, c, :], bank[1][:, c * 256:(c + 1) * 256].rearrange("p (g t) -> p g t", g=B), ACT.Sigmoid,
                      bias=prm[:, P_ATIME + c:P_ATIME + c + 1]).then_inc(S("agate_done"), 1)
                act.wait_ge(S("k_mm"), 1)
                A(kraw[:, :, :, :], gct(bank[3][:, :]), ACT.Copy).then_inc(S("kraw_done"), 1)
                A(ksq[:, :, :], bank[3][:, :], ACT.Square).then_inc(S("ksq_done"), 1)
                act.wait_ge(S("v_mm"), 1)
                A(vt[:, :, :], bank[0][:, :], ACT.Copy).then_inc(S("v_done"), 1)
                act.wait_ge(S("g_A_mm"), 1)
                A(h_g[:], bank[2][:, 0:256], ACT.Tanh).then_inc(S("hg_done"), 1)
                act.wait_ge(S("sig_done"), 2)
                A(rootd[:, :, :, :], sig[:, :, :, :], ACT.Sqrt, scale=math.exp(-0.5)).then_inc(S("rootd_done"), 1)
                act.wait_ge(S("nrm_mm"), 1)
                A(nrm[:, :, :], DB[:, 0:256], ACT.Sqrt).then_inc(S("nrm_done"), 1)
                act.wait_ge(S("gate_mm"), 1)
                A(gate[:, :, :], bank[1][:, :], ACT.Copy).then_inc(S("gate_done"), 1)
                for l in range(LEVELS):
                    todo = list(PIECES[l])

                    def elementwise(piece):
                        kind, p = piece
                        if kind == "lora":
                            relu(1, p)
                        if kind == "diff":
                            relu(2, p)
                    elementwise(todo[0])
                    if l >= 1:
                        inv_tr(l - 1, 0)
                    for piece in todo[1:]:
                        elementwise(piece)
                    if l >= 1:
                        inv_tr(l - 1, 1)
                act.wait_ge(S("nm1_done"), 1)
                for g in range(B):
                    A(e8[:, g, :], lg[:, g, :], ACT.Exp, bias=nm1[:, g:g + 1]).then_inc(S("e8_done"), 1)
                    A(e2[:, g:g + 1], top8[:, g, 1:2], ACT.Exp, bias=nm1[:, g:g + 1]).then_inc(S("e8_done"), 1)
                for g in range(B):
                    act.wait_ge(S("p_mm"), g + 1)
                    A(pp[:, g, :, :], GB[g][:, 0:256], ACT.Copy).then_inc(S("p_done"), 1)
                for g in range(B):
                    act.wait_ge(S("bkt_mm"), g + 1)
                    A(bkt[:, g, :, :, :], DB[:, :], ACT.Copy).then_inc(S("bkt_done"), 1)
                inv_tr(LEVELS - 1, 0)
                inv_tr(LEVELS - 1, 1)
                act.wait_ge(S("ypre_done"), B)
                A(ysg[:, :, :], y1[:, :, :], ACT.Sigmoid).then_inc(S("ysg_done"), 1)
                for g in range(B):
                    act.wait_ge(S("sa_mm"), g + 1)
                    A(sa[:, g, :, :], GB[g][:, 256:512], ACT.Copy).then_inc(S("sa_done"), 1)
                for g in range(B):
                    act.wait_ge(S("y_mm"), g + 1)
                    A(yy[:, g, :, :], CB[g][:, 0:256], ACT.Copy).then_inc(S("y_done"), 1)
                act.wait_ge(S("yc_done"), 1)
                A(ysq[:, :, :], yc[:, :, :], ACT.Square).then_inc(S("ysq_done"), 1)
                act.wait_ge(S("v8_done"), 1)
                A(sd8[:], v8[:], ACT.Sqrt, scale=1.0 / N, bias=eps[:, 1:2]).then_inc(S("sd8_done"), 1)
                act.wait_ge(S("zt_mm"), 1)
                A(zt[:, :, :, :], DB[:, :], ACT.Copy).then_inc(S("zt_done"), 1)
                act.wait_ge(S("zt_done"), 1)
                A(scratch[:, 1:2], zt[:, 0, 0, 0:1], ACT.Copy).then_inc(S("act_end"), 1)

        @block.gpsimd
        def _(pool):
            tt = nc.gpsimd.tensor_tensor
            pool.wait_ge(zeroed, NZ)
            with pool.Fori(0, TILES) as i:
                pool.wait_ge(go, i + 1)
                tt(scratchp[:, 0:1], eps[:, 0:1], eps[:, 0:1], ALU.add)
                for k, q in enumerate(MIX_ORDER):
                    pool.wait_ge(S("miu_read"), 2 * k + 2)
                    tt(xd[:, q, :, :], mtmp[:, k % 2, :, :].rearrange("p c (g t) -> p c g t", g=B),
                       xnc[:, :, :, 1:L + 1], ALU.add).then_inc(S("xd_done"), 1)
                pool.wait_ge(S("r_done"), 1)
                pool.wait_ge(S("bk_ready"), 2)
                for j in range(2):
                    tt(dg[:, j, :, :, :], rr[:, :, :, :], bk[:, :, j, :, :], ALU.mult).then_inc(S("dg_done"), 1)
                pool.wait_ge(S("d_done"), 1)
                for l in range(LEVELS):
                    m = 1 << l
                    for g in range(B):
                        n = (L // 2) >> l
                        tv = tot[l][:, g, :, :].rearrange("p c (n two) -> p (c n) two", two=2)
                        if l:
                            pool.wait_ge(S("tot_done"), 2 * (l - 1) + g + 1)
                        tt(tot[l + 1][:, g, :, :].rearrange("p c n -> p (c n)"), tv[:, :, 0], tv[:, :, 1], ALU.mult)\
                            .then_inc(S("tot_done"), 1)
                        pool.wait_ge(S("g1_mm"), 2 * l + g + 1)
                        if l == 0:
                            pool.wait_ge(S("dg_done"), 2)
                        if l:
                            pool.wait_ge(S("bk_scaled"), 2 * (l - 1) + g + 1)
                        v = bk[:, g, :, :, :].rearrange("p a c (n two m) -> p a (c n) two m", two=2, m=m)[:, :, :, 0, :]
                        tt(v, v, tv[:, :, 1].unsqueeze(1).unsqueeze(3).to_broadcast([128, 2, 2 * n, m]), ALU.mult)\
                            .then_inc(S("bk_scaled"), 1)
                    for kind, p in PIECES[l]:
                        if kind == "diff":
                            pool.wait_ge(S("relu1_done"), 2 * p + 2)
                            pool.wait_ge(S("relu2_done"), 2 * p + 2)
                            if p >= 2:
                                pool.wait_ge(S("down_mm"), p - 1)
                            tt(hid[:, p % 2, :], relu1[:, p % 2, :], relu2[:, p % 2, :], ALU.add)\
                                .then_inc(S("hid_done"), 1)
                pool.wait_ge(S("diag_read"), 5)
                pool.wait_ge(S("v_done"), 1)
                tt(bv[:, :, :, :], vt[:, :, :].rearrange("p g (h n) -> p g h n", n=N),
                   bonus[:, :, :].unsqueeze(3).to_broadcast([128, B, H, N]), ALU.mult).then_inc(S("bv_done"), 1)
                pool.wait_ge(S("bv_done"), 1)
                tt(scratchp[:, 1:2], bv[:, 0, 0, 0:1], bv[:, 0, 0, 0:1], ALU.add).then_inc(S("pool_end"), 1)

        @block.vector
        def _(dve):
            v = nc.vector
            count = {}

            def run(ins, name="dve_step"):
                count[name] = count.get(name, 0) + 1
                ins.then_inc(S(name), 1)
                return name, count[name]

            def need(token):
                dve.wait_ge(S(token[0]), token[1])

            def store(l, g, p):
                m = 1 << l
                n = HALF // m
                dve.wait_ge(S(f"g{p}_mm"), 2 * l + g + 1)
                if l:
                    dve.wait_ge(S(f"g{p}_stored"), 2 * (l - 1) + g + 1)
                else:
                    dve.wait_ge(S("diag_read"), 5)
                src = GB[p][:, :].rearrange("p (x n m) -> p x n m", x=8, m=m)
                dst = gm[:, g, p].rearrange("p k c a (n two m) -> p (k c a) n two m", two=2, m=m)[:, :, :, 1, :]
                msk = mask_g[:, l, :].rearrange("p (n m) -> p n m", m=m).unsqueeze(1)
                if l == 0:
                    dve.wait_ge(S("inv0_done"), g + 1)
                    run(v.copy_predicated(tinvT[:, g, 2 * p:2 * p + 2, :].rearrange("p h (n two) -> p h n two", two=2)[:, :, :, 1],
                                          mask_g[:, 0, :].unsqueeze(1).to_broadcast([128, 2, HALF]),
                                          GB[p][:, 0:256].rearrange("p (h a n) -> p h a n", h=2, a=2)[:, :, 0, :]), "inv1_done")
                run(v.copy_predicated(dst, msk.to_broadcast([128, 8, n, m]), src), f"g{p}_stored")

            def scale_ar(l, g):
                m, n = 1 << l, HALF >> l
                dve.wait_ge(S("g1_mm"), 2 * l + g + 1)
                if l:
                    dve.wait_ge(S("tot_done"), 2 * (l - 1) + g + 1)
                    dve.wait_ge(S("ar_scaled"), 2 * (l - 1) + g + 1)
                tv = tot[l][:, g, :, :].rearrange("p c (n two) -> p (c n) two", two=2)
                a = ar[:, g, :, :, :].rearrange("p a c (n two m) -> p a (c n) two m", two=2, m=m)[:, :, :, 1, :]
                run(v.tensor_tensor(a, a, tv[:, :, 0].unsqueeze(1).unsqueeze(3).to_broadcast([128, 2, 2 * n, m]),
                                    ALU.mult), "ar_scaled")

            def keep_x(l, g):
                dve.wait_ge(S("x_mm"), 2 * (l - 1) + g + 1)
                run(v.tensor_tensor(xb[:, g, :, :], CB[g][:, 0:256].rearrange("p (h n) -> p h n", h=H),
                                    mask_x[:, l, :].unsqueeze(1).to_broadcast([128, H, HALF]), ALU.mult), "x_done")

            def add_off(l, g):
                m = 1 << l
                n = HALF // m
                dve.wait_ge(S("off_mm"), 2 * (l - 1) + g + 1)
                tl = tinv[:, g, :, :].rearrange("p h (n two m) -> p (h n) two m", two=2, m=m)[:, :, 0, :]
                run(v.tensor_tensor(tl, tl, CB[g][:, 256:512].rearrange("p (n m) -> p n m", m=m), ALU.add), "inv_added")

            for buf in (xnc, gm, state):
                v.memset(buf[:], 0.0).then_inc(zeroed, 1)
            v.memset(eps[:, 0:1], EPS_LN).then_inc(zeroed, 1)
            v.memset(eps[:, 1:2], EPS_GN).then_inc(zeroed, 1)
            v.memset(scratch[:], 0.0).then_inc(zeroed, 1)
            dve.wait_ge(zeroed, NZ)
            dve.wait_ge(loaded, 16 * NW)
            with dve.Fori(0, TILES) as i:
                dve.wait_ge(go, i + 1)
                v.memset(scratch[:, 2:3], 0.0)
                for g in range(B):
                    t = run(v.bn_stats(st6[:, g, :], x_in[:, g, :]))
                    need(t)
                    run(v.bn_aggr(mv[:, g, :], st6[:, g, :]), "var_done")
                t = run(v.tensor_copy(xnc[:, :, :, 0], xnc[:, :, :, L]), "carry_done")
                dve.wait_ge(S("std_done"), 1)
                need(run(v.reciprocal(rstd[:, :], rstd[:, :])))
                for g in range(B):
                    run(v.tensor_scalar(xn[:, g, :], x_in[:, g, :], mv[:, g, 0:1], rstd[:, g:g + 1],
                                        ALU.subtract, ALU.mult), "xn_done")
                need(t)
                dve.wait_ge(S("xnc_done"), 1)
                need(run(v.tensor_tensor(dx[:, :, :].rearrange("p c (g t) -> p (c g) t", g=B),
                                         xnc[:, :, :, 0:L].rearrange("p c g t -> p (c g) t"),
                                         xnc[:, :, :, 1:L + 1].rearrange("p c g t -> p (c g) t"), ALU.subtract)))
                for c in range(2):
                    run(v.scalar_tensor_tensor(xm[:, c, :].rearrange("p (g t) -> p g t", g=B),
                                               dx[:, c, :].rearrange("p (g t) -> p g t", g=B),
                                               prm[:, P_XMIU + c:P_XMIU + c + 1], xnc[:, c, :, 1:L + 1],
                                               ALU.mult, ALU.add), "xm_done")
                dve.wait_ge(S("route_mm"), 1)
                route = bank[1][:, 0:272].rearrange("p (g n) -> p g n", g=B)
                need(run(v.tensor_tensor(lg[:, :, :], route[:, :, 128:136],
                                         w["gate_b"][:].unsqueeze(1).to_broadcast([128, B, E]), ALU.add)))
                t = [run(v.max(top8[:, g, :], lg[:, g, :])) for g in range(B)][-1]
                need(t)
                run(v.tensor_scalar(nm1[:, :], top8[:, :, 0], -1.0, None, ALU.mult), "nm1_done")
                for g in range(B):
                    t = run(v.scalar_tensor_tensor(hit[:, g, :], lg[:, g, :], top8[:, g, 0:1], rev8[:], ALU.is_ge, ALU.mult))
                need(t)
                need(run(v.tensor_reduce(hmx[:, :], hit[:, :, :], AX.X, ALU.max)))
                for g in range(B):
                    t = run(v.tensor_scalar(oh1[:, g, :], hit[:, g, :], hmx[:, g:g + 1], None, ALU.is_equal))
                need(t)
                need(run(v.tensor_scalar(rest[:, :, :], oh1[:, :, :], -1.0, 1.0, ALU.mult, ALU.add)))
                for g in range(B):
                    t = run(v.scalar_tensor_tensor(hit[:, g, :], lg[:, g, :], top8[:, g, 1:2], rest[:, g, :],
                                                   ALU.is_ge, ALU.mult))
                need(t)
                need(run(v.tensor_tensor(hit[:, :, :], hit[:, :, :], rev8[:].unsqueeze(1).to_broadcast([128, B, E]), ALU.mult)))
                need(run(v.tensor_reduce(hmx[:, :], hit[:, :, :], AX.X, ALU.max)))
                for g in range(B):
                    t = run(v.tensor_scalar(oh2[:, g, :], hit[:, g, :], hmx[:, g:g + 1], None, ALU.is_equal))
                need(t)
                need(run(v.tensor_tensor(oh2[:, :, :], oh2[:, :, :], oh1[:, :, :], ALU.subtract)))
                for j, o in enumerate((oh1, oh2)):
                    run(v.tensor_tensor(xmask[:, j, :, :].rearrange("p g (e r) -> p g e r", r=RANK),
                                        route[:, :, 0:128].rearrange("p g (e r) -> p g e r", r=RANK),
                                        o[:, :, :].unsqueeze(3).to_broadcast([128, B, E, RANK]), ALU.mult), "xmask_done")
                for k, q in enumerate(MIX_ORDER):
                    dve.wait_ge(S("miu_mm"), k + 1)
                    if k >= 2:
                        dve.wait_ge(S("xd_done"), k - 1)
                    for c in range(2):
                        run(v.scalar_tensor_tensor(mtmp[:, k % 2, c, :], bank[2 + k % 3][:, c * 256:(c + 1) * 256],
                                                   prm[:, P_LAM + 2 * q + c:P_LAM + 2 * q + c + 1], dx[:, c, :],
                                                   ALU.add, ALU.mult), "miu_read")
                dve.wait_ge(S("sig_done"), 2)
                need(run(v.tensor_scalar(tot[0][:, :, :, :], sig[:, :, :, :], math.exp(-0.5), None, ALU.mult), "d_done"))
                dve.wait_ge(S("r_done"), 1)
                run(v.tensor_tensor(ar[:, :, 1, :, :], rr[:, :, :, :], tot[0][:, :, :, :], ALU.mult), "ar_ready")
                dve.wait_ge(S("nrm_done"), 1)
                need(run(v.tensor_scalar(nrm1[:, :, :], nrm[:, :, :], 1e-12, None, ALU.max)))
                need(run(v.reciprocal(kinv[:, :, :], nrm1[:, :, :])))
                dve.wait_ge(S("kraw_done"), 1)
                need(run(v.tensor_tensor(kh[:, :, :, :], kraw[:, :, :, :],
                                         kinv[:, :, :].unsqueeze(2).to_broadcast([128, B, 2, L]), ALU.mult)))
                dve.wait_ge(S("agate_done"), 2)
                run(v.scalar_tensor_tensor(bk[:, :, 0, :, :].rearrange("p g c t -> p g (c t)"),
                                           kh[:, :, :, :].rearrange("p g c t -> p g (c t)"), 2.0,
                                           agate[:, :, :, :].rearrange("p g c t -> p g (c t)"), ALU.mult, ALU.mult), "bk_ready")
                dve.wait_ge(S("rootd_done"), 1)
                run(v.tensor_tensor(bk[:, :, 1, :, :], kh[:, :, :, :], rootd[:, :, :, :], ALU.mult), "bk_ready")
                run(v.tensor_scalar(ar[:, :, 0, :, :], kh[:, :, :, :], -1.0, None, ALU.mult), "ar_ready")
                for c in range(2):
                    run(v.scalar_tensor_tensor(dg[:, 2, :, c, :], rr[:, :, c, :], prm[:, P_XTIME + c:P_XTIME + c + 1],
                                               kh[:, :, c, :], ALU.mult, ALU.mult), "dg2_done")
                dve.wait_ge(S("diag_mm"), 1)
                dgp = DB[:, 0:24].rearrange("p (g j h) -> p g j h", g=B, j=3)
                run(v.tensor_copy(bonus[:, :, :].rearrange("p g (c q) -> p g c q", q=2),
                                  dgp[:, :, 2, :].rearrange("p g (q c) -> p g c q", q=2)), "diag_read")
                for g in range(B):
                    for j in range(2):
                        run(v.copy_predicated(gm[:, g, :, j, :, 1, :],
                                              mask_d[:].unsqueeze(1).unsqueeze(1).to_broadcast([128, 2, 2, L]),
                                              dgp[:, g, j, :].rearrange("p (q c) -> p q c", q=2).unsqueeze(3)
                                              .to_broadcast([128, 2, 2, L])), "diag_read")
                dve.wait_ge(S("ar_ready"), 2)
                for l in range(LEVELS):
                    if l >= 2:
                        keep_x(l - 1, 0)
                        keep_x(l - 1, 1)
                    store(l, 0, 0)
                    store(l, 0, 1)
                    scale_ar(l, 0)
                    if l >= 2:
                        add_off(l - 1, 0)
                    store(l, 1, 0)
                    if l >= 2:
                        add_off(l - 1, 1)
                    store(l, 1, 1)
                    scale_ar(l, 1)
                top = LEVELS - 1
                keep_x(top, 0)
                keep_x(top, 1)
                add_off(top, 0)
                add_off(top, 1)
                dve.wait_ge(S("e8_done"), 2 * B)
                need(run(v.tensor_reduce(esum[:, :], e8[:, :, :], AX.X, ALU.add)))
                need(run(v.reciprocal(esum[:, :], esum[:, :])))
                need(run(v.scalar_tensor_tensor(vsum[:, :], e2[:, :], 1.0, esum[:, :], ALU.add, ALU.mult)))
                dve.wait_ge(S("down_mm"), PAIRS)
                need(run(v.scalar_tensor_tensor(y1[:, :, :], w["bo"][:].unsqueeze(1).to_broadcast([128, B, C]), 2.0,
                                                FB[:, :].rearrange("p (g n) -> p g n", g=B), ALU.mult, ALU.add)))
                for g in range(B):
                    run(v.tensor_scalar(y1[:, g, :], y1[:, g, :], vsum[:, g:g + 1], None, ALU.mult), "ypre_done")
                dve.wait_ge(S("ysg_done"), 1)
                dve.wait_ge(S("ypre_done"), B)
                run(v.tensor_tensor(fgate[:, :, :], y1[:, :, :], ysg[:, :, :], ALU.mult))
                for g in range(B):
                    dve.wait_ge(S("inc_mm"), g + 1)
                    dve.wait_ge(S("tot_done"), 2 * LEVELS)
                    for c in range(2):
                        for o in (0, 64):
                            st = state[o:o + 64, g, c, o:o + 64]
                            run(v.scalar_tensor_tensor(st, st,
                                                       tot[LEVELS][o:o + 64, g, c, :],
                                                       GB[g][o:o + 64, c * 128 + o:c * 128 + o + 64], ALU.mult, ALU.add))
                dve.wait_ge(S("y_done"), B)
                yv = yy[:, :, :, :].rearrange("p g h n -> p (g h) n")
                need(run(v.tensor_reduce(s8[:, :], yv, AX.X, ALU.add)))
                need(run(v.tensor_scalar(mean8[:, :], s8[:, :], 1.0 / N, None, ALU.mult)))
                run(v.tensor_tensor(yc[:, :, :], yv, mean8[:, :].unsqueeze(2).to_broadcast([128, B * H, N]), ALU.subtract), "yc_done")
                dve.wait_ge(S("ysq_done"), 1)
                run(v.tensor_reduce(v8[:, :], ysq[:, :, :], AX.X, ALU.add), "v8_done")
                dve.wait_ge(S("sd8_done"), 1)
                need(run(v.reciprocal(rs8[:, :], sd8[:, :])))
                need(run(v.tensor_tensor(yn[:, :, :].rearrange("p g (h n) -> p (g h) n", n=N), yc[:, :, :],
                                         rs8[:, :].unsqueeze(2).to_broadcast([128, B * H, N]), ALU.mult)))
                need(run(v.tensor_tensor(yn2[:, :, :], yn[:, :, :], w["gamma"][:].unsqueeze(1).to_broadcast([128, B, C]), ALU.mult)))
                need(run(v.tensor_tensor(yn[:, :, :], yn2[:, :, :], w["beta"][:].unsqueeze(1).to_broadcast([128, B, C]), ALU.add)))
                dve.wait_ge(S("bv_done"), 1)
                need(run(v.tensor_tensor(yn2[:, :, :], yn[:, :, :], bv[:, :, :, :].rearrange("p g h n -> p g (h n)"), ALU.add)))
                run(v.tensor_tensor(zz[:, :, :], yn2[:, :, :], gate[:, :, :], ALU.mult), "zz_done")
                dve.wait_ge(S("o_mm"), 1)
                need(run(v.tensor_tensor(of[:, :, :], CB[0][:, :].rearrange("p (g n) -> p g n", g=B), fgate[:, :, :], ALU.mult)))
                run(v.tensor_tensor(out_t[:, :, :], of[:, :, :], x_res[:, :, :], ALU.add), "out_done")

        @block.sync
        def _(sp):
            sp.dma_start(prm[:], par).then_inc(loaded, 16)
            for k, src in list(weights.items()) + list(consts.items()):
                dst = w[k] if k in w else cst[k]
                sp.dma_start(dst[:], src).then_inc(loaded, 16)
            sp.dma_start(x_in[:, :, :], x[0]).then_inc(S("x_loaded"), 16)
            with sp.Fori(0, TILES) as i:
                sp.wait_ge(S("x_loaded"), 16)
                sp.sem_inc(go, 1)
                sp.wait_ge(S("xn_done"), B)
                sp.wait_ge(S("xres_done"), 1)
                sp.dma_start(x_in[:, :, :], x[i + 1]).then_inc(S("x_next"), 16)
                sp.wait_ge(S("out_done"), 1)
                sp.dma_start(out[i], out_t[:, :, :]).then_inc(S("out_stored"), 16)
                sp.wait_ge(S("act_end"), 1)
                sp.wait_ge(S("pool_end"), 1)
                sp.wait_ge(S("x_next"), 16)
                sp.wait_ge(S("out_stored"), 16)
                names = [n for n in sems if n != "x_loaded"]
                for n in names:
                    sp.sem_clear(sems[n])


def kernel(**inputs):
    import numpy as np
    import concourse.bacc as bacc
    from concourse.bass_utils import run_bass_kernel_spmd as run_spmd

    a = {k[3:]: np.asarray(v) for k, v in inputs.items()}

    def halves(m):
        return np.ascontiguousarray(m.reshape(-1, 128, m.shape[-1]).transpose(1, 0, 2))

    def cols(v):
        return v.reshape(-1, 128).T

    par = np.zeros((128, P_COLS), np.float32)
    par[:, P_LAM:P_WMIU] = cols(a["attn_lambdas"])
    par[:, P_WMIU:P_ATIME] = cols(a["attn_w_miu"])
    par[:, P_ATIME:P_XMIU] = cols(a["attn_a_time"])
    par[:, P_XMIU:P_XTIME] = cols(a["attn_x_miu"])
    par[:, P_XTIME:P_BI] = cols(a["attn_x_time"])
    par[:, P_BI:P_COLS] = cols(a["ffn_bi"])
    x_b = np.zeros((128, 2, 256), np.float32)
    x_b[:, 0, :] = a["attn_x_B"][:4].reshape(128, 256)
    x_b[0:64, 1, :] = a["attn_x_B"][4:].reshape(64, 256)
    weights = {
        "x_A": halves(a["attn_x_A"]), "x_B": x_b,
        "w_A": halves(a["attn_w_A"]), "w_B": a["attn_w_B"], "k_A": halves(a["attn_k_A"]), "k_B": a["attn_k_B"],
        "a_A": halves(a["attn_a_A"]), "a_B": a["attn_a_B"], "g_A": halves(a["attn_g_A"]), "g_B": a["attn_g_B"],
        "rW": halves(a["attn_rW"].T), "kW": halves(a["attn_kW"].T), "vW": halves(a["attn_vW"].T), "oW": halves(a["attn_oW"].T),
        "route": halves(np.concatenate([a["ffn_lora_A"].reshape(128, 256).T, a["ffn_gate_w"].T], 1)),
        "wi": halves(a["ffn_wi"].T), "lora_B": a["ffn_lora_B"].transpose(0, 2, 1).reshape(128, 1024),
        "wo": halves(a["ffn_wo"].T),
        "gate_b": np.broadcast_to(a["ffn_gate_b"], (128, 8)), "bo": np.broadcast_to(a["ffn_bo"], (128, 256)),
        "gamma": np.broadcast_to(a["attn_gn_gamma"], (128, 256)), "beta": np.broadcast_to(a["attn_gn_beta"], (128, 256)),
    }
    tok = np.arange(128)
    mask_g = np.zeros((128, LEVELS, HALF), np.int32)
    mask_x = np.zeros((128, LEVELS, HALF), np.float32)
    for l in range(LEVELS):
        m = 1 << l
        lefts = tok[(tok // m) % 2 == 0]
        rights = tok[(tok // m) % 2 == 1]
        for j in range(HALF):
            mask_g[:, l, j] = (tok // (2 * m) == rights[j] // (2 * m)) & ((tok // m) % 2 == 0)
            mask_x[:, l, j] = (tok // (2 * m) == lefts[j] // (2 * m)) & ((tok // m) % 2 == 1)
    consts = {
        "ident": np.eye(128, dtype=np.float32), "ones": np.ones((128, 128), np.float32),
        "headsel": (tok[:, None] // 64 == np.arange(2)[None, :]).astype(np.float32),
        "mask_g": mask_g, "mask_x": mask_x, "mask_d": np.eye(128, dtype=np.int32),
        "rev8": np.broadcast_to(np.arange(8, 0, -1).astype(np.float32), (128, 8)),
    }
    xs = np.zeros((TILES + 1, L, B, C), np.float32)
    xs[:TILES] = a["attn_x"].reshape(B, TILES, L, C).transpose(1, 2, 0, 3)

    nc = bacc.Bacc("TRN2", target_bir_lowering=False, num_devices=1)
    arrays = {}

    def dram(name, arr):
        arrays[name] = np.ascontiguousarray(arr)
        return nc.dram_tensor(name, arr.shape, mybir.dt.from_np(arr.dtype), kind="ExternalInput").ap()

    x_ap, par_ap = dram("x", xs), dram("par", par)
    w_ap = {k: dram("w_" + k + "_dram", v) for k, v in weights.items()}
    c_ap = {k: dram("c_" + k + "_dram", v) for k, v in consts.items()}
    o_ap = nc.dram_tensor("out", (TILES, L, B, C), F32, kind="ExternalOutput").ap()
    program(nc, x_ap, par_ap, w_ap, c_ap, o_ap)
    r = run_spmd(nc, [arrays], core_ids=[0])
    o = r.results[0]["out"]
    return np.ascontiguousarray(o.reshape(TILES, L, B, C).transpose(2, 0, 1, 3).reshape(B, T, C))
```

```python
import concourse.bass as bass
from concourse import mybir
from contextlib import ExitStack
import math

F32 = mybir.dt.float32
I32 = mybir.dt.int32
ALU = mybir.AluOpType
ACT = mybir.ActivationFunctionType
AX = mybir.AxisListType

B, T, C = 2, 2048, 256
H, N = 4, 64
L = 128
TILES = T // L
E, RANK, FF = 8, 16, 1024
LEVELS = int(math.log2(L))
HALF = L // 2
EPS_LN, EPS_GN = 1e-5, 1e-5 * H
R_, W_, K_, V_, A_, G_ = range(6)
MIX_ORDER = [W_, K_, A_, G_, R_, V_]
SLOT = {q: k for k, q in enumerate(MIX_ORDER)}
PAIRS = FF // 256
P_LAM, P_WMIU, P_ATIME, P_XMIU, P_XTIME, P_BI, P_COLS = 0, 12, 14, 16, 18, 20, 28


def program(nc, x, par, weights, consts, out):
    ctx = ExitStack()
    with ctx:
        def sb(name, shape, dt=F32):
            return ctx.enter_context(nc.sbuf_tensor(name, shape, dt))

        sems = {}

        def S(name):
            if name not in sems:
                sems[name] = ctx.enter_context(nc.semaphore(name))
            return sems[name]

        go = ctx.enter_context(nc.semaphore("tile_go"))
        x_first = ctx.enter_context(nc.semaphore("first_x_loaded"))
        loaded = ctx.enter_context(nc.semaphore("weights_loaded"))
        zeroed = ctx.enter_context(nc.semaphore("buffers_zeroed"))

        w = {k: sb("w_" + k, list(v.shape)) for k, v in weights.items()}
        cst = {k: sb("c_" + k, list(v.shape), v.dtype) for k, v in consts.items()}
        prm = sb("prm", [128, P_COLS])
        ident, ones, headsel = cst["ident"], cst["ones"], cst["headsel"]
        mask_g, mask_x, mask_d, rev8 = cst["mask_g"], cst["mask_x"], cst["mask_d"], cst["rev8"]

        x_in = sb("x_in", [128, B, C])
        x_a = sb("x_a", [128, B, C])
        x_b = sb("x_b", [128, B, C])
        st6 = sb("st6", [128, B, 6])
        mv = sb("mv", [128, B, 2])
        rstd = sb("rstd", [128, B])
        eps = sb("eps", [128, 2])
        xn = sb("xn", [128, B, C])
        xnc = sb("xnc", [128, 2, B, L + 1])
        dx = sb("dx", [128, 2, B * L])
        xm = sb("xm", [128, 2, B * L])
        mixt = sb("mixt", [128, 2, B * L])
        mtmp = sb("mtmp", [128, 2, 2, B * L])
        xd = sb("xd", [128, 6, 2, B * L])
        hid = xd[:, 0:PAIRS, :, :].rearrange("p q c t -> p q (c t)")
        lg = sb("lg", [128, B, E])
        top8 = sb("top8", [128, B, 8])
        nm1 = sb("nm1", [128, B])
        e8 = sb("e8", [128, B, E])
        esum = sb("esum", [128, B])
        e2 = sb("e2", [128, B])
        vsum = sb("vsum", [128, B])
        hit = sb("hit", [128, B, E])
        hmx = sb("hmx", [128, B])
        oh1 = sb("oh1", [128, B, E])
        oh2 = sb("oh2", [128, B, E])
        rest = sb("rest", [128, B, E])
        rt = sb("rt", [128, B, 136])
        xmask = sb("xmask", [128, 2, B, 128])
        xmt = sb("xmt", [128, 2, B * L])
        relu1 = sb("relu1", [128, 2, 512])
        relu2 = sb("relu2", [128, 2, 512])
        y1 = sb("y1", [128, B, C])
        ysg = sb("ysg", [128, B, C])
        fgate = sb("fgate", [128, B, C])
        h_w = sb("h_w", [64, B * L])
        h_k = sb("h_k", [64, B * L])
        h_a = sb("h_a", [64, B * L])
        h_g = sb("h_g", [128, B * L])
        sig = sb("sig", [128, B, 2, L])
        rootd = sb("rootd", [128, B, 2, L])
        agate = sb("agate", [128, B, 2, L])
        kraw = sb("kraw", [128, B, 2, L])
        ksq = sb("ksq", [128, 2, B * L])
        nrm = sb("nrm", [128, B, L])
        nrm1 = sb("nrm1", [128, B, L])
        kinv = sb("kinv", [128, B, L])
        rr = sb("rr", [128, B, 2, L])
        kh = sb("kh", [128, B, 2, L])
        vt = sb("vt", [128, B, C])
        v_r = sb("v_r", [128, B, C])
        gate = sb("gate", [128, B, C])
        gate_r = sb("gate_r", [128, B, C])
        dg = sb("dg", [128, 3, B, 2, L])
        bonus = sb("bonus", [128, B, H])
        ar = sb("ar", [128, B, 2, 2, L])
        bk = sb("bk", [128, B, 2, 2, L])
        tot = [sb(f"tot{l}", [128, B, 2, L >> l]) for l in range(LEVELS + 1)]
        gm = sb("gm", [128, B, 2, 2, 2, 2, L])
        tinv = sb("tinv", [128, B, H, L])
        tinvT = sb("tinvT", [128, B, H, L])
        xb = sb("xb", [128, B, H, HALF])
        pp = sb("pp", [128, B, H, N])
        sa = sb("sa", [128, B, H, N])
        bkt = sb("bkt", [128, B, 2, 2, L])
        state = sb("state", [128, B, 2, 2 * N])
        yy = sb("yy", [128, B, H, N])
        s8 = sb("s8", [128, B * H])
        mean8 = sb("mean8", [128, B * H])
        yc = sb("yc", [128, B * H, N])
        ysq = sb("ysq", [128, B * H, N])
        v8 = sb("v8", [128, B * H])
        sd8 = sb("sd8", [128, B * H])
        rs8 = sb("rs8", [128, B * H])
        yn = sb("yn", [128, B, C])
        yn2 = sb("yn2", [128, B, C])
        bv = sb("bv", [128, B, H, N])
        zz = sb("zz", [128, B, C])
        zt = sb("zt", [128, 2, B, L])
        out_t = sb("out_t", [128, B, C])
        scratch = sb("scratch", [128, 4])
        scratchp = sb("scratchp", [128, 4])

        bank = [ctx.enter_context(nc.psum_tensor(f"bank{i}", [128, 512], F32)) for i in range(8)]
        GB, CB, ZB = [bank[0], bank[1]], [bank[2], bank[3]], [bank[5], bank[6]]
        DB, FB = bank[4], bank[7]

        NW = len(weights) + len(consts) + 1
        ZEROED = (xnc, gm, state, yy, bv, gate_r, x_b, fgate)
        NZ = len(ZEROED) + 3
        TOP = LEVELS - 1
        block = ctx.enter_context(nc.Block())

        def slot(h):
            return 2 * (h % 2) + h // 2

        def left(v, m):
            return v.rearrange("p (n two m) -> p n two m", two=2, m=m)[:, :, 0, :]

        def gct(psum):
            return psum.rearrange("p (c g t) -> p g c t", c=2, g=B)

        BEFORE = [[], [], ["mix"], ["miu01"], ["miu23", "o"], ["a_A"], ["r", "a_B"]]
        AFTER = [["xt"], [], [], ["zt"], ["w_A", "k_A", "miu45"], ["w_B", "kW"], ["xmt", "k_B", "v", "g_A"]]
        BETWEEN = [[], ["route"], [], [], [], [], []]
        POST = ("zt", "o")
        FFN_INV = [("base", 0), ("base", 1)]
        FFN_TR = [("lora", 0)]
        FFN_SA = [("lora", 1)]
        FFN_Y = [("diff", 0), ("diff", 1), ("diag", 0), ("base", 2), ("lora", 2), ("diag", 1), ("down", 0), ("base", 3),
                 ("lora", 3), ("diff", 2), ("diff", 3), ("down", 1)]
        LATE = [("down", 2), ("down", 3)]

        @block.tensor
        def _(pe):
            mm = nc.tensor.matmul
            tr = nc.tensor.transpose

            def ffn(kind, p, rec):
                z = ZB[p % 2]
                if kind == "base":
                    if p == 0:
                        pe.wait_ge(S("v_done"), 1)
                    if p == 1:
                        pe.wait_ge(S("hg_done"), 1)
                    if p >= 2:
                        pe.wait_ge(S("relu2_done"), 2 * (p - 2) + 2)
                    for j in range(2):
                        for c in range(2):
                            f = (2 * p + j) * 128
                            mm(z[:, j * 256:(j + 1) * 256], w["wi"][:, c, f:f + 128], xnc[:, c, :, 1:L + 1],
                               start=(j == 0 and c == 0), stop=False, skip_group_check=True)
                if kind in ("lora", "diff"):
                    e = 0 if kind == "lora" else 1
                    if kind == "lora":
                        pe.wait_ge(S("xmt_done"), 1)
                    else:
                        pe.wait_ge(S("relu1_done"), 2 * p + 2)
                    for j in range(2):
                        f = (2 * p + j) * 128
                        last = mm(z[:, j * 256:(j + 1) * 256], w["lora_B"][:, f:f + 128], xmt[:, e, :],
                                  start=False, stop=True, skip_group_check=True)
                    last.then_inc(S("z1_mm" if kind == "lora" else "z2_mm"), 1)
                if kind == "down":
                    if p < 2:
                        pe.wait_ge(S("hid_done"), p + 1)
                    if p == 0:
                        pe.wait_ge(S("gate_done"), 1)
                    for j in range(2):
                        for g in range(B):
                            f = 2 * p + j
                            last = mm(FB[:, g * C:(g + 1) * C], hid[:, p, j * 256 + g * L:j * 256 + (g + 1) * L],
                                      w["wo"][:, f, :], start=(f == 0 and g == 0), stop=(f == 2 * PAIRS - 1),
                                      skip_group_check=True)
                    last.then_inc(S("down_mm" if p < 2 else "down_late_mm"), 1)
                if kind == "diag":
                    if p == 0:
                        pe.wait_ge(S("dg_done"), 2)
                        pe.wait_ge(S("dg2_done"), 2)
                        pe.wait_ge(S("nrm_done"), 1)
                    if p == 0 and rec:
                        pe.wait_ge(S("bkt_done"), 2)
                    for j in range(3):
                        for c in range(2):
                            o = (p * 3 + j) * H + c
                            last = mm(DB[:, o:o + 3:2], dg[:, j, p, c, :], headsel[:], start=True, stop=True)
                    last.then_inc(S("diag_mm"), 1)

            def low(dst, name, q, m):
                pe.wait_ge(S("xd_done"), SLOT[q] + 1)
                for c in range(2):
                    last = mm(dst[0:m, 0:B * L], w[name][:, c, :], xd[:, q, c, :], start=(c == 0), stop=(c == 1))
                last.then_inc(S(name + "_mm"), 1)

            def to_channels(dst, src, name):
                for c in range(2):
                    for g in range(B):
                        last = tr(dst[:, (c * B + g) * L:(c * B + g + 1) * L], src[:, g, c * 128:(c + 1) * 128], ident[:])
                last.then_inc(S(name), 1)

            def piece(name, front, rec):
                if name == "xt":
                    pe.wait_ge(S("xn_done"), B)
                    to_channels(bank[4], xn, "xt_mm")
                if name == "route":
                    pe.wait_ge(S("xnc_done"), 1)
                    for g in range(B):
                        for c in range(2):
                            last = mm(bank[5][:, g * 136:(g + 1) * 136], xnc[:, c, g, 1:L + 1], w["route"][:, c, :],
                                      start=(c == 0), stop=(c == 1))
                    last.then_inc(S("route_mm"), 1)
                if name == "mix":
                    pe.wait_ge(S("xm_done"), 2)
                    if rec:
                        pe.wait_ge(S("y1_read"), 1)
                    for u, m in ((0, 128), (1, 64)):
                        for c in range(2):
                            last = mm(bank[7][0:m, u * 256:(u + 1) * 256], w["x_A"][:, c, u * 128:u * 128 + m], xm[:, c, :],
                                      start=(c == 0), stop=(c == 1))
                    last.then_inc(S("mix_mm"), 1)
                if name.startswith("miu"):
                    ks = [int(k) for k in name[3:]]
                    if ks[0] == 0:
                        pe.wait_ge(S("mixt_done"), 2)
                    else:
                        pe.wait_ge(S("miu_read"), 2 * ks[0])
                    if ks[0] == 2 and rec:
                        pe.wait_ge(S("zt_done"), 1)
                    for c in range(2):
                        for k in ks:
                            q = MIX_ORDER[k]
                            o, u = 32 * (q % 4), q // 4
                            last = mm(bank[4 + 2 * (k % 2)][:, c * 256:(c + 1) * 256],
                                      w["x_B"][o:o + 32, u, c * 128:(c + 1) * 128], mixt[o:o + 32, u, :], start=True, stop=True)
                    last.then_inc(S("miu_mm"), 1)
                if name == "xmt":
                    pe.wait_ge(S("agate_done"), 2)
                    pe.wait_ge(S("xmask_done"), 2)
                    for j in range(2):
                        for g in range(B):
                            last = tr(bank[7][:, (j * B + g) * L:(j * B + g + 1) * L], xmask[:, j, g, :], ident[:])
                    last.then_inc(S("xmt_mm"), 1)
                if name == "w_A":
                    pe.wait_ge(S("mixt_done"), 2)
                    low(bank[7], "w_A", W_, 64)
                if name == "k_A":
                    pe.wait_ge(S("route_read"), 1)
                    if rec:
                        pe.wait_ge(S("o_read"), 1)
                    low(bank[5], "k_A", K_, 64)
                if name == "a_A":
                    pe.wait_ge(S("hw_done"), 1)
                    low(bank[7], "a_A", A_, 64)
                if name == "w_B":
                    pe.wait_ge(S("hk_done"), 1)
                    for c in range(2):
                        last = mm(bank[5][:, c * 256:(c + 1) * 256], w["w_B"][0:64, c * 128:(c + 1) * 128], h_w[:],
                                  start=True, stop=True)
                    last.then_inc(S("w_B_mm"), 1)
                if name == "kW":
                    pe.wait_ge(S("miu_read"), 10)
                    for c in range(2):
                        for k in range(2):
                            mm(bank[4][:, c * 256:(c + 1) * 256], w["kW"][:, k, c * 128:(c + 1) * 128], xd[:, K_, k, :],
                               start=(c == 0 and k == 0), stop=False, skip_group_check=True)
                if name == "r":
                    pe.wait_ge(S("xd_done"), SLOT[R_] + 1)
                    pe.wait_ge(S("miu_read"), 12)
                    for c in range(2):
                        for k in range(2):
                            last = mm(bank[6][:, c * 256:(c + 1) * 256], w["rW"][:, k, c * 128:(c + 1) * 128],
                                      xd[:, R_, k, :], start=(k == 0), stop=(k == 1))
                    last.then_inc(S("r_mm"), 1)
                if name == "a_B":
                    pe.wait_ge(S("ha_done"), 1)
                    for c in range(2):
                        last = mm(bank[7][:, c * 256:(c + 1) * 256], w["a_B"][0:64, c * 128:(c + 1) * 128], h_a[:],
                                  start=True, stop=True)
                    last.then_inc(S("a_B_mm"), 1)
                if name == "k_B":
                    pe.wait_ge(S("hk_done"), 1)
                    for c in range(2):
                        last = mm(bank[4][:, c * 256:(c + 1) * 256], w["k_B"][0:64, c * 128:(c + 1) * 128], h_k[:],
                                  start=False, stop=True, skip_group_check=True)
                    last.then_inc(S("k_mm"), 1)
                if name == "v":
                    pe.wait_ge(S("xd_done"), SLOT[V_] + 1)
                    pe.wait_ge(S("sig_done"), 2)
                    for g in range(B):
                        for k in range(2):
                            last = mm(bank[5][:, g * C:(g + 1) * C], xd[:, V_, k, g * L:(g + 1) * L], w["vW"][:, k, :],
                                      start=(k == 0), stop=(k == 1))
                    last.then_inc(S("v_mm"), 1)
                if name == "g_A":
                    pe.wait_ge(S("r_done"), 1)
                    low(bank[6], "g_A", G_, 128)
                if name == "norm":
                    pe.wait_ge(S("ksq_done"), 1)
                    for c in range(2):
                        last = mm(DB[:, 0:B * L], ones[:], ksq[:, c, :], start=(c == 0), stop=(c == 1))
                    last.then_inc(S("nrm_mm"), 1)
                if name == "g_B":
                    pe.wait_ge(S("hg_done"), 1)
                    pe.wait_ge(S("xmt_done"), 1)
                    for g in range(B):
                        last = mm(bank[7][:, g * C:(g + 1) * C], h_g[:, g * L:(g + 1) * L], w["g_B"][:], start=True, stop=True)
                    last.then_inc(S("gate_mm"), 1)
                if name == "zt":
                    pe.wait_ge(S("zz_done"), 1)
                    if front:
                        pe.wait_ge(S("miu_read"), 4)
                    to_channels(bank[6], zz, "zt_mm")
                if name == "o":
                    pe.wait_ge(S("zt_done"), 1)
                    if front:
                        pe.wait_ge(S("route_read"), 1)
                    for g in range(B):
                        for c in range(2):
                            last = mm(bank[5][:, g * C:(g + 1) * C], zt[:, c, g, :], w["oW"][:, c, :],
                                      start=(c == 0), stop=(c == 1))
                    last.then_inc(S("o_mm"), 1)

            def gram(l, g):
                n, m = 2 * l + g, 1 << l
                if l:
                    pe.wait_ge(S("ar_scaled"), 2 * (l - 1) + g + 1)
                    pe.wait_ge(S("bk_scaled"), 2 * (l - 1) + g + 1)
                if n:
                    pe.wait_ge(S("g0_stored"), n)
                    pe.wait_ge(S("g1_stored"), n)
                for kind in range(2):
                    for c in range(2):
                        for p in range(2):
                            o = 64 * p
                            rhs = ar[o:o + 64, g, :, c, :].rearrange("p a (n two m) -> p a n two m", two=2, m=m)[:, :, :, 1, :]
                            last = mm(GB[p][:, (2 * kind + c) * 128:(2 * kind + c + 1) * 128], bk[o:o + 64, g, kind, c, :],
                                      rhs, start=True, stop=True)
                last.then_inc(S("g_mm"), 1)

            def inv_x(l, g):
                pe.wait_ge(S("tr_done"), 2 * (l - 1) + g + 1)
                pe.wait_ge(S("g0_stored"), 2 * l + g + 1)
                pe.wait_ge(S("g1_stored"), 2 * l + g + 1)
                for h in range(H):
                    last = mm(CB[g][:, h * HALF:(h + 1) * HALF], gm[:, g, h // 2, 0, h % 2, 0, :],
                              left(tinv[:, g, h, :], 1 << l), start=True, stop=True)
                last.then_inc(S("x_mm"), 1)

            def inv_off(l, g):
                pe.wait_ge(S("x_done"), 2 * (l - 1) + g + 1)
                for h in range(H):
                    last = mm(CB[g][:, 256 + h * HALF:256 + (h + 1) * HALF], tinvT[:, g, h, :], xb[:, g, h, :],
                              start=True, stop=True)
                last.then_inc(S("off_mm"), 1)

            def inv_tr(l, g):
                if l == 0:
                    pe.wait_ge(S("inv1_done"), 2 * g + 2)
                else:
                    pe.wait_ge(S("inv_added"), 2 * (l - 1) + g + 1)
                for h in range(H):
                    last = tr(CB[g][:, h * L:(h + 1) * L], (tinvT if l == 0 else tinv)[:, g, h, :], ident[:])
                last.then_inc(S("tr_mm"), 1)

            def keys_to_tokens(g):
                pe.wait_ge(S("bk_scaled"), 2 * TOP + g + 1)
                if g:
                    pe.wait_ge(S("bkt_done"), g)
                for j in range(2):
                    for c in range(2):
                        last = tr(DB[:, (j * 2 + c) * L:(j * 2 + c + 1) * L], bk[:, g, j, c, :], ident[:])
                last.then_inc(S("bkt_mm"), 1)

            def tile(step, front, rec, post):
                def pieces(names):
                    for name in names:
                        if post if name in POST else front:
                            piece(name, front, rec)

                def feed(todo):
                    if front:
                        for kind, p in todo:
                            ffn(kind, p, rec)

                pe.wait_ge(go, step)
                mm(bank[6][:, 0:128], ident[:], ident[:], start=True, stop=True)
                if rec:
                    ffn(*LATE[0], rec)
                for l in range(LEVELS):
                    pieces(BEFORE[l])
                    if rec:
                        if l >= 2:
                            inv_x(l - 1, 0)
                        gram(l, 0)
                        if l == 0:
                            ffn(*LATE[1], rec)
                        if l == 1:
                            inv_tr(0, 0)
                            inv_tr(0, 1)
                        if l >= 2:
                            inv_x(l - 1, 1)
                            inv_off(l - 1, 0)
                    pieces(BETWEEN[l])
                    if rec:
                        gram(l, 1)
                        if l >= 2:
                            inv_off(l - 1, 1)
                    pieces(AFTER[l])
                    if rec and l >= 2:
                        inv_tr(l - 1, 0)
                        inv_tr(l - 1, 1)
                if rec:
                    inv_x(TOP, 0)
                    inv_x(TOP, 1)
                pieces(["norm", "g_B"])
                if rec:
                    for g in range(B):
                        pe.wait_ge(S("ar_scaled"), 2 * TOP + g + 1)
                        pe.wait_ge(S("g0_stored"), 2 * LEVELS)
                        pe.wait_ge(S("g1_stored"), 2 * LEVELS)
                        if g == 0:
                            pe.wait_ge(S("vr_done"), 1)
                        for c in range(2):
                            mm(GB[g][:, c * 128:(c + 1) * 128], ar[:, g, 0, c, :], state[:, g, c, :], start=True, stop=False,
                               skip_group_check=True)
                            for h in (2 * c, 2 * c + 1):
                                last = mm(GB[g][:, h * N:(h + 1) * N], gm[:, g, h % 2, 1, c, 0, :],
                                          v_r[:, g, h * N:(h + 1) * N], start=False, stop=True, skip_group_check=True)
                        last.then_inc(S("p_mm"), 1)
                    inv_off(TOP, 0)
                    inv_off(TOP, 1)
                feed(FFN_INV)
                if rec:
                    if front:
                        pe.wait_ge(S("nrm_done"), 1)
                    keys_to_tokens(0)
                    inv_tr(TOP, 0)
                    inv_tr(TOP, 1)
                feed(FFN_TR)
                if rec:
                    keys_to_tokens(1)
                    for g in range(B):
                        pe.wait_ge(S("tr_done"), 2 * TOP + g + 1)
                        pe.wait_ge(S("p_done"), g + 1)
                        for h in range(H):
                            last = mm(GB[g][:, 256 + h * N:256 + (h + 1) * N], tinvT[:, g, slot(h), :], pp[:, g, h, :],
                                      start=True, stop=True)
                        last.then_inc(S("sa_mm"), 1)
                feed(FFN_SA)
                if rec:
                    for g in range(B):
                        pe.wait_ge(S("sa_done"), g + 1)
                        for c in range(2):
                            mm(CB[g][:, c * 128:(c + 1) * 128], ar[:, g, 1, c, :], state[:, g, c, :], start=True, stop=False,
                               skip_group_check=True)
                            for h in (2 * c, 2 * c + 1):
                                dst = CB[g][:, h * N:(h + 1) * N]
                                mm(dst, gm[:, g, h % 2, 0, c, 1, :], sa[:, g, h, :], start=False, stop=False,
                                   skip_group_check=True)
                                last = mm(dst, gm[:, g, h % 2, 1, c, 1, :], v_r[:, g, h * N:(h + 1) * N], start=False,
                                          stop=True, skip_group_check=True)
                        last.then_inc(S("y_mm"), 1)
                        pe.wait_ge(S("bkt_done"), g + 1)
                        for c in range(2):
                            dst = GB[g][:, c * 128:(c + 1) * 128]
                            mm(dst, bkt[:, g, 0, c, :], sa[:, g, 2 * c:2 * c + 2, :], start=True, stop=False)
                            last = mm(dst, bkt[:, g, 1, c, :], v_r[:, g, c * 128:(c + 1) * 128], start=False, stop=True)
                        last.then_inc(S("inc_mm"), 1)
                feed(FFN_Y)

            pe.wait_ge(loaded, 16 * NW)
            pe.wait_ge(zeroed, NZ)
            tile(1, True, False, False)
            with pe.Fori(0, TILES - 1) as i:
                tile(i + 2, True, True, True)
            tile(TILES + 1, False, True, True)
            tile(TILES + 2, False, False, True)

        @block.scalar
        def _(act):
            A = nc.scalar.activation

            def relu(which, p):
                act.wait_ge(S(f"z{which}_mm"), p + 1)
                if p >= 2:
                    act.wait_ge(S("hid_done"), p - 1)
                dst = relu1 if which == 1 else relu2
                for j in range(2):
                    A(dst[:, p % 2, j * 256:(j + 1) * 256], ZB[p % 2][:, j * 256:(j + 1) * 256], ACT.Relu,
                      bias=prm[:, P_BI + 2 * p + j:P_BI + 2 * p + j + 1]).then_inc(S(f"relu{which}_done"), 1)

            def inv_tr(l, g):
                act.wait_ge(S("tr_mm"), 2 * l + g + 1)
                dst = tinv if l == 0 else tinvT
                A(dst[:, g, :, :], CB[g][:, :], ACT.Copy).then_inc(S("tr_done"), 1)

            def biased_sigmoid(dst, src, col, name):
                for c in range(2):
                    A(dst[:, :, c, :], src[:, c * 256:(c + 1) * 256].rearrange("p (g t) -> p g t", g=B), ACT.Sigmoid,
                      bias=prm[:, col + c:col + c + 1]).then_inc(S(name), 1)

            def piece(name, rec):
                if name == "xt":
                    act.wait_ge(S("xt_mm"), 1)
                    act.wait_ge(S("carry_done"), 1)
                    A(xnc[:, :, :, 1:L + 1], bank[4][:, :].rearrange("p (c g t) -> p c g t", c=2, g=B), ACT.Copy)\
                        .then_inc(S("xnc_done"), 1)
                if name == "route":
                    act.wait_ge(S("route_mm"), 1)
                    A(rt[:, :, :], bank[5][:, 0:272], ACT.Copy).then_inc(S("route_read"), 1)
                if name == "mix":
                    act.wait_ge(S("mix_mm"), 1)
                    A(mixt[:, 0, :], bank[7][:, 0:256], ACT.Tanh).then_inc(S("mixt_done"), 1)
                    A(mixt[0:64, 1, :], bank[7][0:64, 256:512], ACT.Tanh).then_inc(S("mixt_done"), 1)
                if name == "xmt":
                    act.wait_ge(S("xmt_mm"), 1)
                    A(xmt[:, :, :], bank[7][:, :], ACT.Copy).then_inc(S("xmt_done"), 1)
                if name == "w_A":
                    act.wait_ge(S("w_A_mm"), 1)
                    A(h_w[:], bank[7][0:64, 0:256], ACT.Tanh).then_inc(S("hw_done"), 1)
                if name == "k_A":
                    act.wait_ge(S("k_A_mm"), 1)
                    A(h_k[:], bank[5][0:64, 0:256], ACT.Tanh).then_inc(S("hk_done"), 1)
                    act.wait_ge(S("nm1_done"), 1)
                    for g in range(B):
                        A(e8[:, g, :], lg[:, g, :], ACT.Exp, bias=nm1[:, g:g + 1]).then_inc(S("e8_done"), 1)
                        A(e2[:, g:g + 1], top8[:, g, 1:2], ACT.Exp, bias=nm1[:, g:g + 1]).then_inc(S("e8_done"), 1)
                if name == "a_A":
                    act.wait_ge(S("a_A_mm"), 1)
                    A(h_a[:], bank[7][0:64, 0:256], ACT.Copy).then_inc(S("ha_done"), 1)
                if name == "w_B":
                    act.wait_ge(S("w_B_mm"), 1)
                    biased_sigmoid(sig, bank[5], P_WMIU, "sig_done")
                if name == "r":
                    act.wait_ge(S("r_mm"), 1)
                    A(rr[:, :, :, :], gct(bank[6][:, :]), ACT.Copy).then_inc(S("r_done"), 1)
                if name == "a_B":
                    act.wait_ge(S("a_B_mm"), 1)
                    biased_sigmoid(agate, bank[7], P_ATIME, "agate_done")
                if name == "k_B":
                    act.wait_ge(S("k_mm"), 1)
                    A(kraw[:, :, :, :], gct(bank[4][:, :]), ACT.Copy).then_inc(S("kraw_done"), 1)
                    A(ksq[:, :, :], bank[4][:, :], ACT.Square).then_inc(S("ksq_done"), 1)
                if name == "v":
                    act.wait_ge(S("v_mm"), 1)
                    if rec:
                        act.wait_ge(S("vr_done"), 1)
                    A(vt[:, :, :], bank[5][:, :], ACT.Copy).then_inc(S("v_done"), 1)
                if name == "g_A":
                    act.wait_ge(S("g_A_mm"), 1)
                    A(h_g[:], bank[6][:, 0:256], ACT.Tanh).then_inc(S("hg_done"), 1)
                if name == "norm":
                    act.wait_ge(S("nrm_mm"), 1)
                    A(nrm[:, :, :], DB[:, 0:256], ACT.Sqrt).then_inc(S("nrm_done"), 1)
                    act.wait_ge(S("sig_done"), 2)
                    A(rootd[:, :, :, :], sig[:, :, :, :], ACT.Sqrt, scale=math.exp(-0.5)).then_inc(S("rootd_done"), 1)
                if name == "g_B":
                    act.wait_ge(S("gate_mm"), 1)
                    if rec:
                        act.wait_ge(S("gate_moved"), 1)
                    A(gate[:, :, :], bank[7][:, :], ACT.Copy).then_inc(S("gate_done"), 1)
                if name == "zt":
                    act.wait_ge(S("zt_mm"), 1)
                    A(zt[:, :, :, :], bank[6][:, :], ACT.Copy).then_inc(S("zt_done"), 1)

            def tile(step, front, rec, post):
                def pieces(names):
                    for name in names:
                        if post if name in POST else front:
                            piece(name, rec)

                def feed(todo):
                    if front:
                        for kind, p in todo:
                            if kind == "lora":
                                relu(1, p)
                            if kind == "diff":
                                relu(2, p)

                act.wait_ge(go, step)
                A(scratch[:, 0:1], eps[:, 0:1], ACT.Copy)
                if front:
                    act.wait_ge(S("var_done"), B)
                    A(rstd[:, :], mv[:, :, 1], ACT.Sqrt, bias=eps[:, 0:1]).then_inc(S("std_done"), 1)
                if rec:
                    A(v_r[:, :, :], vt[:, :, :], ACT.Copy).then_inc(S("vr_done"), 1)
                for l in range(LEVELS):
                    pieces(BEFORE[l])
                    if l == 1 and post:
                        act.wait_ge(S("v8_done"), 1)
                        A(sd8[:], v8[:], ACT.Sqrt, scale=1.0 / N, bias=eps[:, 1:2]).then_inc(S("sd8_done"), 1)
                    if rec and l == 1:
                        inv_tr(0, 0)
                        inv_tr(0, 1)
                    pieces(BETWEEN[l])
                    pieces(AFTER[l])
                    if l == 0 and post:
                        act.wait_ge(S("yc_done"), 1)
                        A(ysq[:, :, :], yc[:, :, :], ACT.Square).then_inc(S("ysq_done"), 1)
                    if rec and l >= 2:
                        inv_tr(l - 1, 0)
                        inv_tr(l - 1, 1)
                    if l == 4 and rec:
                        if post:
                            act.wait_ge(S("zz_done"), 1)
                            act.wait_ge(S("out_done"), 1)
                        A(gate_r[:, :, :], gate[:, :, :], ACT.Copy).then_inc(S("gate_moved"), 1)
                        A(x_b[:, :, :], x_a[:, :, :], ACT.Copy).then_inc(S("xb_moved"), 1)
                    if l == 4 and front:
                        if rec:
                            act.wait_ge(S("xb_moved"), 1)
                        A(x_a[:, :, :], x_in[:, :, :], ACT.Copy).then_inc(S("xa_moved"), 1)
                    if l == 5 and rec:
                        act.wait_ge(S("ypre_done"), B)
                        A(ysg[:, :, :], y1[:, :, :], ACT.Sigmoid).then_inc(S("ysg_done"), 1)
                pieces(["norm", "g_B"])
                if rec:
                    for g in range(B):
                        act.wait_ge(S("p_mm"), g + 1)
                        A(pp[:, g, :, :], GB[g][:, 0:256], ACT.Copy).then_inc(S("p_done"), 1)
                feed(FFN_INV)
                if rec:
                    act.wait_ge(S("bkt_mm"), 1)
                    A(bkt[:, 0, :, :, :], DB[:, :], ACT.Copy).then_inc(S("bkt_done"), 1)
                    inv_tr(TOP, 0)
                    inv_tr(TOP, 1)
                feed(FFN_TR)
                if rec:
                    act.wait_ge(S("bkt_mm"), 2)
                    A(bkt[:, 1, :, :, :], DB[:, :], ACT.Copy).then_inc(S("bkt_done"), 1)
                    for g in range(B):
                        act.wait_ge(S("sa_mm"), g + 1)
                        A(sa[:, g, :, :], GB[g][:, 256:512], ACT.Copy).then_inc(S("sa_done"), 1)
                feed(FFN_SA)
                if rec:
                    for g in range(B):
                        act.wait_ge(S("y_mm"), g + 1)
                        if g == 0 and post:
                            act.wait_ge(S("yc_done"), 1)
                        A(yy[:, g, :, :], CB[g][:, 0:256], ACT.Copy).then_inc(S("y_done"), 1)
                if front:
                    if rec:
                        act.wait_ge(S("y_mm"), B)
                    act.wait_ge(S("kh_done"), 1)
                    A(ar[:, :, 0, :, :], kh[:, :, :, :], ACT.Copy, scale=-1.0).then_inc(S("ar0_ready"), 1)
                    for g in range(B):
                        A(tinvT[:, g, :, :], ident[:].unsqueeze(1).to_broadcast([128, H, L]), ACT.Copy)\
                            .then_inc(S("inv0_done"), 1)
                feed(FFN_Y)
                A(scratch[:, 1:2], eps[:, 0:1], ACT.Copy).then_inc(S("act_end"), 1)

            act.wait_ge(loaded, 16 * NW)
            act.wait_ge(zeroed, NZ)
            tile(1, True, False, False)
            with act.Fori(0, TILES - 1) as i:
                tile(i + 2, True, True, True)
            tile(TILES + 1, False, True, True)
            tile(TILES + 2, False, False, True)

        @block.gpsimd
        def _(pool):
            tt = nc.gpsimd.tensor_tensor

            def mixed(k, rec):
                q = MIX_ORDER[k]
                pool.wait_ge(S("miu_read"), 2 * k + 2)
                if k == 0 and rec:
                    pool.wait_ge(S("down_late_mm"), 2)
                tt(xd[:, q, :, :], mtmp[:, k % 2, :, :].rearrange("p c (g t) -> p c g t", g=B),
                   xnc[:, :, :, 1:L + 1], ALU.add).then_inc(S("xd_done"), 1)

            def scale_bk(l, g):
                m, n = 1 << l, HALF >> l
                tv = tot[l][:, g, :, :].rearrange("p c (n two) -> p (c n) two", two=2)
                if l:
                    pool.wait_ge(S("tot_done"), 2 * (l - 1) + g + 1)
                tt(tot[l + 1][:, g, :, :].rearrange("p c n -> p (c n)"), tv[:, :, 0], tv[:, :, 1], ALU.mult)\
                    .then_inc(S("tot_done"), 1)
                pool.wait_ge(S("g_mm"), 2 * l + g + 1)
                if l:
                    pool.wait_ge(S("bk_scaled"), 2 * (l - 1) + g + 1)
                v = bk[:, g, :, :, :].rearrange("p a c (n two m) -> p a (c n) two m", two=2, m=m)[:, :, :, 0, :]
                tt(v, v, tv[:, :, 1].unsqueeze(1).unsqueeze(3).to_broadcast([128, 2, 2 * n, m]), ALU.mult)\
                    .then_inc(S("bk_scaled"), 1)

            def tile(step, front, rec, post):
                def pieces(names):
                    for name in names:
                        if front and name.startswith("miu"):
                            for k in name[3:]:
                                mixed(int(k), rec)

                pool.wait_ge(go, step)
                tt(scratchp[:, 0:1], eps[:, 0:1], eps[:, 0:1], ALU.add)
                for l in range(LEVELS):
                    pieces(BEFORE[l])
                    if rec:
                        scale_bk(l, 0)
                        scale_bk(l, 1)
                    if l == 4 and rec:
                        if post:
                            pool.wait_ge(S("zz_done"), 1)
                        pool.wait_ge(S("vr_done"), 1)
                        tt(bv[:, :, :, :], v_r[:, :, :].rearrange("p g (h n) -> p g h n", n=N),
                           bonus[:, :, :].unsqueeze(3).to_broadcast([128, B, H, N]), ALU.mult).then_inc(S("bv_done"), 1)
                        pool.wait_ge(S("bv_done"), 1)
                        tt(bv[:, :, :, :].rearrange("p g h n -> p g (h n)"), bv[:, :, :, :].rearrange("p g h n -> p g (h n)"),
                           w["beta"][:].unsqueeze(1).to_broadcast([128, B, C]), ALU.add).then_inc(S("bv_shifted"), 1)
                    pieces(AFTER[l])
                if front:
                    pool.wait_ge(S("kh_done"), 1)
                    pool.wait_ge(S("rootd_done"), 1)
                    if rec:
                        pool.wait_ge(S("bkt_mm"), B)
                    tt(bk[:, :, 1, :, :], kh[:, :, :, :], rootd[:, :, :, :], ALU.mult).then_inc(S("bk1_ready"), 1)
                    pool.wait_ge(S("bk1_ready"), 1)
                    pool.wait_ge(S("r_done"), 1)
                    tt(dg[:, 1, :, :, :], rr[:, :, :, :], bk[:, :, 1, :, :], ALU.mult).then_inc(S("dg_done"), 1)
                    pool.wait_ge(S("bk0_ready"), 1)
                    tt(dg[:, 0, :, :, :], rr[:, :, :, :], bk[:, :, 0, :, :], ALU.mult).then_inc(S("dg_done"), 1)
                tt(scratchp[:, 1:2], eps[:, 0:1], eps[:, 0:1], ALU.add).then_inc(S("pool_end"), 1)

            pool.wait_ge(zeroed, NZ)
            tile(1, True, False, False)
            with pool.Fori(0, TILES - 1) as i:
                tile(i + 2, True, True, True)
            tile(TILES + 1, False, True, True)
            tile(TILES + 2, False, False, True)

        @block.vector
        def _(dve):
            v = nc.vector
            count = {}

            def run(ins, name="dve_step"):
                count[name] = count.get(name, 0) + 1
                ins.then_inc(S(name), 1)
                return name, count[name]

            def need(token):
                dve.wait_ge(S(token[0]), token[1])

            def store(l, g, p):
                m = 1 << l
                n = HALF // m
                dve.wait_ge(S("g_mm"), 2 * l + g + 1)
                if l:
                    dve.wait_ge(S(f"g{p}_stored"), 2 * (l - 1) + g + 1)
                src = GB[p][:, :].rearrange("p (x n m) -> p x n m", x=8, m=m)
                dst = gm[:, g, p].rearrange("p k c a (n two m) -> p (k c a) n two m", two=2, m=m)[:, :, :, 1, :]
                msk = mask_g[:, l, :].rearrange("p (n m) -> p n m", m=m).unsqueeze(1)
                if l == 0:
                    run(v.copy_predicated(tinvT[:, g, 2 * p:2 * p + 2, :].rearrange("p h (n two) -> p h n two", two=2)[:, :, :, 1],
                                          mask_g[:, 0, :].unsqueeze(1).to_broadcast([128, 2, HALF]),
                                          GB[p][:, 0:256].rearrange("p (h a n) -> p h a n", h=2, a=2)[:, :, 0, :]), "inv1_done")
                run(v.copy_predicated(dst, msk.to_broadcast([128, 8, n, m]), src), f"g{p}_stored")

            def scale_ar(l, g):
                m, n = 1 << l, HALF >> l
                dve.wait_ge(S("g_mm"), 2 * l + g + 1)
                if l:
                    dve.wait_ge(S("tot_done"), 2 * (l - 1) + g + 1)
                    dve.wait_ge(S("ar_scaled"), 2 * (l - 1) + g + 1)
                tv = tot[l][:, g, :, :].rearrange("p c (n two) -> p (c n) two", two=2)
                a = ar[:, g, :, :, :].rearrange("p a c (n two m) -> p a (c n) two m", two=2, m=m)[:, :, :, 1, :]
                run(v.tensor_tensor(a, a, tv[:, :, 0].unsqueeze(1).unsqueeze(3).to_broadcast([128, 2, 2 * n, m]),
                                    ALU.mult), "ar_scaled")

            def keep_x(l, g):
                dve.wait_ge(S("x_mm"), 2 * (l - 1) + g + 1)
                run(v.tensor_tensor(xb[:, g, :, :], CB[g][:, 0:256].rearrange("p (h n) -> p h n", h=H),
                                    mask_x[:, l, :].unsqueeze(1).to_broadcast([128, H, HALF]), ALU.mult), "x_done")

            def add_off(l, g):
                m = 1 << l
                dve.wait_ge(S("off_mm"), 2 * (l - 1) + g + 1)
                tl = tinv[:, g, :, :].rearrange("p h (n two m) -> p (h n) two m", two=2, m=m)[:, :, 0, :]
                run(v.tensor_tensor(tl, tl, CB[g][:, 256:512].rearrange("p (n m) -> p n m", m=m), ALU.add), "inv_added")

            def router(stage):
                if stage == 0:
                    dve.wait_ge(S("route_read"), 1)
                    need(run(v.tensor_tensor(lg[:, :, :], rt[:, :, 128:136],
                                             w["gate_b"][:].unsqueeze(1).to_broadcast([128, B, E]), ALU.add)))
                    t = [run(v.max(top8[:, g, :], lg[:, g, :])) for g in range(B)][-1]
                    need(t)
                    run(v.tensor_scalar(nm1[:, :], top8[:, :, 0], -1.0, None, ALU.mult), "nm1_done")
                    for g in range(B):
                        t = run(v.scalar_tensor_tensor(hit[:, g, :], lg[:, g, :], top8[:, g, 0:1], rev8[:],
                                                       ALU.is_ge, ALU.mult))
                    need(t)
                    need(run(v.tensor_reduce(hmx[:, :], hit[:, :, :], AX.X, ALU.max)))
                    for g in range(B):
                        run(v.tensor_scalar(oh1[:, g, :], hit[:, g, :], hmx[:, g:g + 1], None, ALU.is_equal), "oh1_done")
                if stage == 1:
                    need(("oh1_done", B))
                    need(run(v.tensor_scalar(rest[:, :, :], oh1[:, :, :], -1.0, 1.0, ALU.mult, ALU.add)))
                    for g in range(B):
                        t = run(v.scalar_tensor_tensor(hit[:, g, :], lg[:, g, :], top8[:, g, 1:2], rest[:, g, :],
                                                       ALU.is_ge, ALU.mult))
                    need(t)
                    need(run(v.tensor_tensor(hit[:, :, :], hit[:, :, :], rev8[:].unsqueeze(1).to_broadcast([128, B, E]),
                                             ALU.mult)))
                    need(run(v.tensor_reduce(hmx[:, :], hit[:, :, :], AX.X, ALU.max)))
                    for g in range(B):
                        run(v.tensor_scalar(oh2[:, g, :], hit[:, g, :], hmx[:, g:g + 1], None, ALU.is_equal), "oh2_done")
                if stage == 2:
                    need(("oh2_done", B))
                    need(run(v.tensor_tensor(oh2[:, :, :], oh2[:, :, :], oh1[:, :, :], ALU.subtract)))
                    for j, o in enumerate((oh1, oh2)):
                        run(v.tensor_tensor(xmask[:, j, :, :].rearrange("p g (e r) -> p g e r", r=RANK),
                                            rt[:, :, 0:128].rearrange("p g (e r) -> p g e r", r=RANK),
                                            o[:, :, :].unsqueeze(3).to_broadcast([128, B, E, RANK]), ALU.mult), "xmask_done")

            def hidden(p):
                dve.wait_ge(S("relu1_done"), 2 * p + 2)
                dve.wait_ge(S("relu2_done"), 2 * p + 2)
                if p == 0:
                    dve.wait_ge(S("g_A_mm"), 1)
                run(v.tensor_tensor(hid[:, p, :], relu1[:, p % 2, :], relu2[:, p % 2, :], ALU.add), "hid_done")

            def gate_sum():
                dve.wait_ge(S("e8_done"), 2 * B)
                need(run(v.tensor_reduce(esum[:, :], e8[:, :, :], AX.X, ALU.add)))
                need(run(v.reciprocal(esum[:, :], esum[:, :])))
                need(run(v.scalar_tensor_tensor(vsum[:, :], e2[:, :], 1.0, esum[:, :], ALU.add, ALU.mult)))

            def mixed(k):
                q = MIX_ORDER[k]
                dve.wait_ge(S("miu_mm"), k // 2 + 1)
                if k >= 2:
                    dve.wait_ge(S("xd_done"), k - 1)
                for c in range(2):
                    run(v.scalar_tensor_tensor(mtmp[:, k % 2, c, :], bank[4 + 2 * (k % 2)][:, c * 256:(c + 1) * 256],
                                               prm[:, P_LAM + 2 * q + c:P_LAM + 2 * q + c + 1], dx[:, c, :],
                                               ALU.add, ALU.mult), "miu_read")

            yv = yy[:, :, :, :].rearrange("p g h n -> p (g h) n")

            def tile(step, front, rec, post):
                count.clear()

                def pieces(names):
                    for name in names:
                        if name.startswith("miu") and front:
                            for k in name[3:]:
                                mixed(int(k))
                        if name == "o" and post:
                            dve.wait_ge(S("o_mm"), 1)
                            need(run(v.tensor_tensor(out_t[:, :, :], bank[5][:, :].rearrange("p (g n) -> p g n", g=B),
                                                     fgate[:, :, :], ALU.mult), "o_read"))
                            run(v.tensor_tensor(out_t[:, :, :], out_t[:, :, :], x_b[:, :, :], ALU.add), "out_done")

                dve.wait_ge(go, step)
                v.memset(scratch[:, 2:3], 0.0)
                if front:
                    for g in range(B):
                        need(run(v.bn_stats(st6[:, g, :], x_in[:, g, :])))
                        run(v.bn_aggr(mv[:, g, :], st6[:, g, :]), "var_done")
                    carried = run(v.tensor_copy(xnc[:, :, :, 0], xnc[:, :, :, L]), "carry_done")
                for l in range(LEVELS):
                    pieces(BEFORE[l])
                    if l == 2 and post:
                        dve.wait_ge(S("sd8_done"), 1)
                        need(run(v.reciprocal(rs8[:, :], sd8[:, :])))
                        run(v.tensor_tensor(yn[:, :, :].rearrange("p g (h n) -> p (g h) n", n=N), yc[:, :, :],
                                            rs8[:, :].unsqueeze(2).to_broadcast([128, B * H, N]), ALU.mult), "yn_done")
                        need(("yn_done", 1))
                        run(v.tensor_tensor(yn2[:, :, :], yn[:, :, :], w["gamma"][:].unsqueeze(1).to_broadcast([128, B, C]),
                                            ALU.mult), "yn_scaled")
                    if rec:
                        if l >= 2:
                            keep_x(l - 1, 0)
                        store(l, 0, 0)
                        store(l, 0, 1)
                        scale_ar(l, 0)
                        if l >= 2:
                            keep_x(l - 1, 1)
                            add_off(l - 1, 0)
                    if l == 0 and front:
                        dve.wait_ge(S("std_done"), 1)
                        need(run(v.reciprocal(rstd[:, :], rstd[:, :])))
                        for g in range(B):
                            run(v.tensor_scalar(xn[:, g, :], x_in[:, g, :], mv[:, g, 0:1], rstd[:, g:g + 1],
                                                ALU.subtract, ALU.mult), "xn_done")
                    if l == 1 and rec:
                        dve.wait_ge(S("down_late_mm"), 2)
                        need(run(v.scalar_tensor_tensor(y1[:, :, :], w["bo"][:].unsqueeze(1).to_broadcast([128, B, C]), 2.0,
                                                        FB[:, :].rearrange("p (g n) -> p g n", g=B), ALU.mult, ALU.add), "y1_read"))
                        for g in range(B):
                            run(v.tensor_scalar(y1[:, g, :], y1[:, g, :], vsum[:, g:g + 1], None, ALU.mult), "ypre_done")
                    if l == 1 and front:
                        need(carried)
                        dve.wait_ge(S("xnc_done"), 1)
                        need(run(v.tensor_tensor(dx[:, :, :].rearrange("p c (g t) -> p (c g) t", g=B),
                                                 xnc[:, :, :, 0:L].rearrange("p c g t -> p (c g) t"),
                                                 xnc[:, :, :, 1:L + 1].rearrange("p c g t -> p (c g) t"), ALU.subtract)))
                        for c in range(2):
                            run(v.scalar_tensor_tensor(xm[:, c, :].rearrange("p (g t) -> p g t", g=B),
                                                       dx[:, c, :].rearrange("p (g t) -> p g t", g=B),
                                                       prm[:, P_XMIU + c:P_XMIU + c + 1], xnc[:, c, :, 1:L + 1],
                                                       ALU.mult, ALU.add), "xm_done")
                    if l == 1 and post:
                        dve.wait_ge(S("ysq_done"), 1)
                        run(v.tensor_reduce(v8[:, :], ysq[:, :, :], AX.X, ALU.add), "v8_done")
                    if rec:
                        store(l, 1, 0)
                        store(l, 1, 1)
                        scale_ar(l, 1)
                        if l >= 2:
                            add_off(l - 1, 1)
                    if l == 0 and post:
                        need(run(v.tensor_reduce(s8[:, :], yv, AX.X, ALU.add)))
                        need(run(v.tensor_scalar(mean8[:, :], s8[:, :], 1.0 / N, None, ALU.mult)))
                        run(v.tensor_tensor(yc[:, :, :], yv, mean8[:, :].unsqueeze(2).to_broadcast([128, B * H, N]),
                                            ALU.subtract), "yc_done")
                    if l == 2 and post:
                        need(("yn_scaled", 1))
                        need(run(v.tensor_tensor(yn[:, :, :], yn2[:, :, :], bv[:, :, :, :].rearrange("p g h n -> p g (h n)"),
                                                 ALU.add)))
                        run(v.tensor_tensor(zz[:, :, :], yn[:, :, :], gate_r[:, :, :], ALU.mult), "zz_done")
                    if l in (3, 4, 5) and front:
                        router(l - 3)
                    pieces(AFTER[l])
                    if l == 5 and front:
                        gate_sum()
                    if l == 5 and rec:
                        dve.wait_ge(S("ysg_done"), 1)
                        if post:
                            dve.wait_ge(S("o_read"), 1)
                        run(v.tensor_tensor(fgate[:, :, :], y1[:, :, :], ysg[:, :, :], ALU.mult), "fgate_done")
                    if l == 6 and front:
                        dve.wait_ge(S("sig_done"), 2)
                        if rec:
                            dve.wait_ge(S("tot_done"), 4)
                        run(v.tensor_scalar(tot[0][:, :, :, :], sig[:, :, :, :], math.exp(-0.5), None, ALU.mult), "d_done")
                if rec:
                    keep_x(TOP, 0)
                    keep_x(TOP, 1)
                    add_off(TOP, 0)
                    add_off(TOP, 1)
                if front:
                    dve.wait_ge(S("nrm_done"), 1)
                    need(run(v.tensor_scalar(nrm1[:, :, :], nrm[:, :, :], 1e-12, None, ALU.max)))
                    need(run(v.reciprocal(kinv[:, :, :], nrm1[:, :, :])))
                    dve.wait_ge(S("kraw_done"), 1)
                    need(run(v.tensor_tensor(kh[:, :, :, :], kraw[:, :, :, :],
                                             kinv[:, :, :].unsqueeze(2).to_broadcast([128, B, 2, L]), ALU.mult), "kh_done"))
                    dve.wait_ge(S("r_done"), 1)
                    for c in range(2):
                        run(v.scalar_tensor_tensor(dg[:, 2, :, c, :], rr[:, :, c, :], prm[:, P_XTIME + c:P_XTIME + c + 1],
                                                   kh[:, :, c, :], ALU.mult, ALU.mult), "dg2_done")
                    if rec:
                        dve.wait_ge(S("bkt_mm"), B)
                    dve.wait_ge(S("agate_done"), 2)
                    run(v.scalar_tensor_tensor(bk[:, :, 0, :, :].rearrange("p g c t -> p g (c t)"),
                                               kh[:, :, :, :].rearrange("p g c t -> p g (c t)"), 2.0,
                                               agate[:, :, :, :].rearrange("p g c t -> p g (c t)"), ALU.mult, ALU.mult),
                        "bk0_ready")
                if rec:
                    dve.wait_ge(S("tot_done"), 2 * LEVELS)
                    for g in range(B):
                        dve.wait_ge(S("inc_mm"), g + 1)
                        for c in range(2):
                            for o in (0, 64):
                                st = state[o:o + 64, g, c, o:o + 64]
                                run(v.scalar_tensor_tensor(st, st, tot[LEVELS][o:o + 64, g, c, :],
                                                           GB[g][o:o + 64, c * 128 + o:c * 128 + o + 64], ALU.mult, ALU.add))
                if front:
                    need(("d_done", 1))
                    run(v.tensor_tensor(ar[:, :, 1, :, :], rr[:, :, :, :], tot[0][:, :, :, :], ALU.mult), "ar1_ready")
                    hidden(0)
                    hidden(1)
                    dve.wait_ge(S("diag_mm"), B)
                    if rec:
                        dve.wait_ge(S("bv_done"), 1)
                    dgp = DB[:, 0:24].rearrange("p (g j h) -> p g j h", g=B, j=3)
                    run(v.tensor_copy(bonus[:, :, :].rearrange("p g (c q) -> p g c q", q=2),
                                      dgp[:, :, 2, :].rearrange("p g (q c) -> p g c q", q=2)), "diag_read")
                    for g in range(B):
                        for j in range(2):
                            run(v.copy_predicated(gm[:, g, :, j, :, 1, :],
                                                  mask_d[:].unsqueeze(1).unsqueeze(1).to_broadcast([128, 2, 2, L]),
                                                  dgp[:, g, j, :].rearrange("p (q c) -> p q c", q=2).unsqueeze(3)
                                                  .to_broadcast([128, 2, 2, L])), "diag_read")
                    hidden(2)
                    hidden(3)
                run(v.memset(scratch[:, 2:3], 0.0), "dve_end")

            for buf in ZEROED:
                v.memset(buf[:], 0.0).then_inc(zeroed, 1)
            v.memset(eps[:, 0:1], EPS_LN).then_inc(zeroed, 1)
            v.memset(eps[:, 1:2], EPS_GN).then_inc(zeroed, 1)
            v.memset(scratch[:], 0.0).then_inc(zeroed, 1)
            dve.wait_ge(zeroed, NZ)
            dve.wait_ge(loaded, 16 * NW)
            tile(1, True, False, False)
            with dve.Fori(0, TILES - 1) as i:
                tile(i + 2, True, True, True)
            tile(TILES + 1, False, True, True)
            tile(TILES + 2, False, False, True)

        @block.sync
        def _(sp):
            sp.dma_start(x_in[:, :, :], x[0]).then_inc(x_first, 16)
            sp.dma_start(prm[:], par).then_inc(loaded, 16)
            for k, src in list(weights.items()) + list(consts.items()):
                dst = w[k] if k in w else cst[k]
                sp.dma_start(dst[:], src).then_inc(loaded, 16)
            sp.wait_ge(x_first, 16)

            S("x_loaded"), S("out_stored")
            nums = [s.num for s in sems.values()]
            assert len(nums) == max(nums) - min(nums) + 1

            def tile(front, rec, post, x_next, out_now):
                sp.sem_inc(go, 1)
                if front:
                    sp.wait_ge(S("xn_done"), B)
                    sp.wait_ge(S("xa_moved"), 1)
                    sp.dma_start(x_in[:, :, :], x_next).then_inc(S("x_loaded"), 16)
                if post:
                    sp.wait_ge(S("out_done"), 1)
                    sp.dma_start(out_now, out_t[:, :, :]).then_inc(S("out_stored"), 16)
                if front:
                    sp.wait_ge(S("down_mm"), 2)
                    sp.wait_ge(S("x_loaded"), 16)
                if rec:
                    sp.wait_ge(S("inc_mm"), B)
                if post:
                    sp.wait_ge(S("o_mm"), 1)
                    sp.wait_ge(S("out_stored"), 16)
                for e in ("act", "pool", "dve"):
                    sp.wait_ge(S(e + "_end"), 1)
                sp.sem_clear(range(min(nums), max(nums) + 1))

            tile(True, False, False, x[1], None)
            with sp.Fori(0, TILES - 1) as i:
                tile(True, True, True, x[i + 2], out[i])
            tile(False, True, True, None, out[TILES - 1])
            tile(False, False, True, None, out[TILES])


def kernel(**inputs):
    import numpy as np
    import concourse.bacc as bacc
    from concourse.bass_utils import run_bass_kernel_spmd as run_spmd

    a = {k[3:]: np.asarray(v) for k, v in inputs.items()}

    def halves(m):
        return np.ascontiguousarray(m.reshape(-1, 128, m.shape[-1]).transpose(1, 0, 2))

    def cols(v):
        return v.reshape(-1, 128).T

    par = np.zeros((128, P_COLS), np.float32)
    par[:, P_LAM:P_WMIU] = cols(a["attn_lambdas"])
    par[:, P_WMIU:P_ATIME] = cols(a["attn_w_miu"])
    par[:, P_ATIME:P_XMIU] = cols(a["attn_a_time"])
    par[:, P_XMIU:P_XTIME] = cols(a["attn_x_miu"])
    par[:, P_XTIME:P_BI] = cols(a["attn_x_time"])
    par[:, P_BI:P_COLS] = cols(a["ffn_bi"])
    x_b = np.zeros((128, 2, 256), np.float32)
    x_b[:, 0, :] = a["attn_x_B"][:4].reshape(128, 256)
    x_b[0:64, 1, :] = a["attn_x_B"][4:].reshape(64, 256)
    weights = {
        "x_A": halves(a["attn_x_A"]), "x_B": x_b,
        "w_A": halves(a["attn_w_A"]), "w_B": a["attn_w_B"], "k_A": halves(a["attn_k_A"]), "k_B": a["attn_k_B"],
        "a_A": halves(a["attn_a_A"]), "a_B": a["attn_a_B"], "g_A": halves(a["attn_g_A"]), "g_B": a["attn_g_B"],
        "rW": halves(a["attn_rW"].T), "kW": halves(a["attn_kW"].T), "vW": halves(a["attn_vW"].T), "oW": halves(a["attn_oW"].T),
        "route": halves(np.concatenate([a["ffn_lora_A"].reshape(128, 256).T, a["ffn_gate_w"].T], 1)),
        "wi": halves(a["ffn_wi"].T), "lora_B": a["ffn_lora_B"].transpose(0, 2, 1).reshape(128, 1024),
        "wo": halves(a["ffn_wo"].T),
        "gate_b": np.broadcast_to(a["ffn_gate_b"], (128, 8)), "bo": np.broadcast_to(a["ffn_bo"], (128, 256)),
        "gamma": np.broadcast_to(a["attn_gn_gamma"], (128, 256)), "beta": np.broadcast_to(a["attn_gn_beta"], (128, 256)),
    }
    tok = np.arange(128)
    mask_g = np.zeros((128, LEVELS, HALF), np.int32)
    mask_x = np.zeros((128, LEVELS, HALF), np.float32)
    for l in range(LEVELS):
        m = 1 << l
        lefts = tok[(tok // m) % 2 == 0]
        rights = tok[(tok // m) % 2 == 1]
        for j in range(HALF):
            mask_g[:, l, j] = (tok // (2 * m) == rights[j] // (2 * m)) & ((tok // m) % 2 == 0)
            mask_x[:, l, j] = (tok // (2 * m) == lefts[j] // (2 * m)) & ((tok // m) % 2 == 1)
    consts = {
        "ident": np.eye(128, dtype=np.float32), "ones": np.ones((128, 128), np.float32),
        "headsel": (tok[:, None] // 64 == np.arange(2)[None, :]).astype(np.float32),
        "mask_g": mask_g, "mask_x": mask_x, "mask_d": np.eye(128, dtype=np.int32),
        "rev8": np.broadcast_to(np.arange(8, 0, -1).astype(np.float32), (128, 8)),
    }
    xs = np.zeros((TILES + 1, L, B, C), np.float32)
    xs[:TILES] = a["attn_x"].reshape(B, TILES, L, C).transpose(1, 2, 0, 3)

    nc = bacc.Bacc("TRN2", target_bir_lowering=False, num_devices=1)
    arrays = {}

    def dram(name, arr):
        arrays[name] = np.ascontiguousarray(arr)
        return nc.dram_tensor(name, arr.shape, mybir.dt.from_np(arr.dtype), kind="ExternalInput").ap()

    x_ap, par_ap = dram("x", xs), dram("par", par)
    w_ap = {k: dram("w_" + k + "_dram", v) for k, v in weights.items()}
    c_ap = {k: dram("c_" + k + "_dram", v) for k, v in consts.items()}
    o_ap = nc.dram_tensor("out", (TILES + 1, L, B, C), F32, kind="ExternalOutput").ap()
    program(nc, x_ap, par_ap, w_ap, c_ap, o_ap)
    r = run_spmd(nc, [arrays], core_ids=[0])
    o = r.results[0]["out"][1:]
    return np.ascontiguousarray(o.reshape(TILES, L, B, C).transpose(2, 0, 1, 3).reshape(B, T, C))
```

```python
import concourse.bass as bass
from concourse import mybir
from contextlib import ExitStack
import math

F32 = mybir.dt.float32
I32 = mybir.dt.int32
ALU = mybir.AluOpType
ACT = mybir.ActivationFunctionType
AX = mybir.AxisListType

B, T, C = 2, 2048, 256
H, N = 4, 64
L = 128
TILES = T // L
E, RANK, FF = 8, 16, 1024
LEVELS = int(math.log2(L))
HALF = L // 2
EPS_LN, EPS_GN = 1e-5, 1e-5 * H
R_, W_, K_, V_, A_, G_ = range(6)
MIX_ORDER = [W_, K_, A_, G_, R_, V_]
SLOT = {q: k for k, q in enumerate(MIX_ORDER)}
PAIRS = FF // 256
P_LAM, P_WMIU, P_ATIME, P_XMIU, P_XTIME, P_BI, P_COLS = 0, 12, 14, 16, 18, 20, 28


def program(nc, x, par, weights, consts, out):
    ctx = ExitStack()
    with ctx:
        def sb(name, shape, dt=F32):
            return ctx.enter_context(nc.sbuf_tensor(name, shape, dt))

        sems = {}

        def S(name):
            if name not in sems:
                sems[name] = ctx.enter_context(nc.semaphore(name))
            return sems[name]

        go = ctx.enter_context(nc.semaphore("tile_go"))
        x_first = ctx.enter_context(nc.semaphore("first_x_loaded"))
        loaded_by = [ctx.enter_context(nc.semaphore(f"weights_loaded_{i}")) for i in range(3)]
        zeroed = ctx.enter_context(nc.semaphore("buffers_zeroed"))
        zeroed_late = ctx.enter_context(nc.semaphore("big_buffers_zeroed"))

        w = {k: sb("w_" + k, list(v.shape)) for k, v in weights.items()}
        cst = {k: sb("c_" + k, list(v.shape), v.dtype) for k, v in consts.items()}
        prm = sb("prm", [128, P_COLS])
        ident, ones, headsel = cst["ident"], cst["ones"], cst["headsel"]
        mask_g, mask_x, mask_d, rev8 = cst["mask_g"], cst["mask_x"], cst["mask_d"], cst["rev8"]

        x_in = sb("x_in", [128, B, C])
        x_a = sb("x_a", [128, B, C])
        x_b = sb("x_b", [128, B, C])
        st6 = sb("st6", [128, B, 6])
        mv = sb("mv", [128, B, 2])
        rstd = sb("rstd", [128, B])
        eps = sb("eps", [128, 2])
        xn = sb("xn", [128, B, C])
        xnc = sb("xnc", [128, 2, B, L + 1])
        dx = sb("dx", [128, 2, B * L])
        xm = sb("xm", [128, 2, B * L])
        mixt = sb("mixt", [128, 2, B * L])
        mtmp = sb("mtmp", [128, 2, 2, B * L])
        xd = sb("xd", [128, 6, 2, B * L])
        hid = xd[:, 0:PAIRS, :, :].rearrange("p q c t -> p q (c t)")
        lg = sb("lg", [128, B, E])
        top8 = sb("top8", [128, B, 8])
        nm1 = sb("nm1", [128, B])
        e8 = sb("e8", [128, B, E])
        esum = sb("esum", [128, B])
        e2 = sb("e2", [128, B])
        vsum = sb("vsum", [128, B])
        hit = sb("hit", [128, B, E])
        hmx = sb("hmx", [128, B])
        oh1 = sb("oh1", [128, B, E])
        oh2 = sb("oh2", [128, B, E])
        rest = sb("rest", [128, B, E])
        rt = sb("rt", [128, B, 136])
        xmask = sb("xmask", [128, 2, B, 128])
        xmt = sb("xmt", [128, 2, B * L])
        relu1 = sb("relu1", [128, 2, 512])
        relu2 = sb("relu2", [128, 2, 512])
        y1 = sb("y1", [128, B, C])
        ysg = sb("ysg", [128, B, C])
        fgate = sb("fgate", [128, B, C])
        h_w = sb("h_w", [64, B * L])
        h_k = sb("h_k", [64, B * L])
        h_a = sb("h_a", [64, B * L])
        h_g = sb("h_g", [128, B * L])
        sig = sb("sig", [128, B, 2, L])
        rootd = sb("rootd", [128, B, 2, L])
        agate = sb("agate", [128, B, 2, L])
        kraw = sb("kraw", [128, B, 2, L])
        ksq = sb("ksq", [128, 2, B * L])
        ksum = sb("ksum", [128, B * L])
        nrm = sb("nrm", [128, B, L])
        nrm1 = sb("nrm1", [128, B, L])
        kinv = sb("kinv", [128, B, L])
        rr = sb("rr", [128, B, 2, L])
        kh = sb("kh", [128, B, 2, L])
        vt = sb("vt", [128, B, C])
        v_r = sb("v_r", [128, B, C])
        gate = sb("gate", [128, B, C])
        gate_r = sb("gate_r", [128, B, C])
        dg = sb("dg", [128, 3, B, 2, L])
        bonus = sb("bonus", [128, B, H])
        ar = sb("ar", [128, B, 2, 2, L])
        bk = sb("bk", [128, B, 2, 2, L])
        bkp = sb("bkp", [128, B, 2, 2, HALF])
        tot = [sb(f"tot{l}", [128, B, 2, L >> l]) for l in range(LEVELS + 1)]
        gm = sb("gm", [128, B, 2, 2, 2, 2, L])
        tinv = sb("tinv", [128, B, H, L])
        tinvT = sb("tinvT", [128, B, H, L])
        xb = sb("xb", [128, B, H, HALF])
        pp = sb("pp", [128, B, H, N])
        sa = sb("sa", [128, B, H, N])
        bkt = sb("bkt", [128, B, 2, 2, L])
        state = sb("state", [128, B, 2, 2 * N])
        yy = sb("yy", [128, B, H, N])
        s8 = sb("s8", [128, B * H])
        mean8 = sb("mean8", [128, B * H])
        yc = sb("yc", [128, B * H, N])
        ysq = sb("ysq", [128, B * H, N])
        v8 = sb("v8", [128, B * H])
        sd8 = sb("sd8", [128, B * H])
        rs8 = sb("rs8", [128, B * H])
        yn = sb("yn", [128, B, C])
        yn2 = sb("yn2", [128, B, C])
        bv = sb("bv", [128, B, H, N])
        zz = sb("zz", [128, B, C])
        zt = sb("zt", [128, 2, B, L])
        out_t = sb("out_t", [128, B, C])
        scratch = sb("scratch", [128, 4])
        scratchp = sb("scratchp", [128, 4])

        bank = [ctx.enter_context(nc.psum_tensor(f"bank{i}", [128, 512], F32)) for i in range(8)]
        GB, CB, ZB = [bank[0], bank[1]], [bank[2], bank[3]], [bank[5], bank[6]]
        DB, FB = bank[4], bank[7]
        DIAG = [bank[4], bank[3]]

        FIRST = ["ident", "route", "gate_b", "x_A", "rev8"]
        SECOND = ["x_B", "w_A", "k_A", "a_A", "w_B", "a_B", "kW", "k_B", "rW", "vW", "g_A", "g_B", "ones", "headsel"]
        names = list(weights) + list(consts)
        GROUPS = [FIRST, SECOND, [k for k in names if k not in FIRST + SECOND]]

        def wait_loaded(engine, i):
            engine.wait_ge(loaded_by[i], 16 * (len(GROUPS[i]) + (i == 0)))

        ZEROED_LATE = (gm, state, zz, x_b, fgate)
        NZ = 4
        TOP = LEVELS - 1
        PACKED = int(math.log2(32))
        block = ctx.enter_context(nc.Block())

        def slot(h):
            return 2 * (h % 2) + h // 2

        def left(v, m):
            return v.rearrange("p (n two m) -> p n two m", two=2, m=m)[:, :, 0, :]

        def gct(psum):
            return psum.rearrange("p (c g t) -> p g c t", c=2, g=B)

        BEFORE = [["zt"], [], [], [], [], [], ["a_B", "kW", "r"]]
        BETWEEN = [[], ["xt"], [], [], [], [], []]
        AFTER = [["o"], ["route"], ["mix"], ["miu01"], ["w_A", "miu23", "k_A"], ["a_A", "miu45", "w_B"], ["xmt", "k_B", "v", "g_A"]]
        POST = ("zt", "o")
        FFN_INV = [("base", 0), ("base", 1)]
        FFN_TR = [("lora", 0)]
        FFN_SA = [("lora", 1)]
        FFN_Y = [("diff", 0), ("diff", 1), ("diag", 0), ("base", 2), ("lora", 2), ("down", 0), ("base", 3), ("lora", 3),
                 ("diff", 2), ("diag", 1), ("diff", 3), ("down", 1)]
        LATE = [("down", 2), ("down", 3)]

        @block.tensor
        def _(pe):
            mm = nc.tensor.matmul
            tr = nc.tensor.transpose

            def ffn(kind, p, rec):
                z = ZB[p % 2]
                if kind == "base":
                    if p == 0:
                        pe.wait_ge(S("v_done"), 1)
                    if p == 1:
                        pe.wait_ge(S("hg_done"), 1)
                    if p >= 2:
                        pe.wait_ge(S("relu2_done"), 2 * (p - 2) + 2)
                    for j in range(2):
                        for c in range(2):
                            f = (2 * p + j) * 128
                            mm(z[:, j * 256:(j + 1) * 256], w["wi"][:, c, f:f + 128], xnc[:, c, :, 1:L + 1],
                               start=(j == 0 and c == 0), stop=False, skip_group_check=True)
                if kind in ("lora", "diff"):
                    e = 0 if kind == "lora" else 1
                    if kind == "lora":
                        pe.wait_ge(S("xmt_done"), 1)
                    else:
                        pe.wait_ge(S("relu1_done"), 2 * p + 2)
                    for j in range(2):
                        f = (2 * p + j) * 128
                        last = mm(z[:, j * 256:(j + 1) * 256], w["lora_B"][:, f:f + 128], xmt[:, e, :],
                                  start=False, stop=True, skip_group_check=True)
                    last.then_inc(S("z1_mm" if kind == "lora" else "z2_mm"), 1)
                if kind == "down":
                    if p < 2:
                        pe.wait_ge(S("hid_done"), p + 1)
                    if p == 0:
                        pe.wait_ge(S("gate_done"), 1)
                    for j in range(2):
                        for g in range(B):
                            f = 2 * p + j
                            last = mm(FB[:, g * C:(g + 1) * C], hid[:, p, j * 256 + g * L:j * 256 + (g + 1) * L],
                                      w["wo"][:, f, :], start=(f == 0 and g == 0), stop=(f == 2 * PAIRS - 1),
                                      skip_group_check=True)
                    last.then_inc(S("down_mm" if p < 2 else "down_late_mm"), 1)
                if kind == "diag":
                    if p == 0:
                        pe.wait_ge(S("dg_done"), 2)
                        pe.wait_ge(S("dg2_done"), 2)
                        pe.wait_ge(S("nrm_done"), 1)
                    if p == 0 and rec:
                        pe.wait_ge(S("bkt_done"), 2)
                    if p == 1 and rec:
                        pe.wait_ge(S("y_done"), B)
                    for j in range(3):
                        for c in range(2):
                            o = j * H + c
                            last = mm(DIAG[p][:, o:o + 3:2], dg[:, j, p, c, :], headsel[:], start=True, stop=True)
                    last.then_inc(S("diag_mm"), 1)

            def low(dst, name, q, m):
                pe.wait_ge(S("xd_done"), SLOT[q] + 1)
                for c in range(2):
                    last = mm(dst[0:m, 0:B * L], w[name][:, c, :], xd[:, q, c, :], start=(c == 0), stop=(c == 1))
                last.then_inc(S(name + "_mm"), 1)

            def to_channels(dst, src, name):
                for c in range(2):
                    for g in range(B):
                        last = tr(dst[:, (c * B + g) * L:(c * B + g + 1) * L], src[:, g, c * 128:(c + 1) * 128], ident[:])
                last.then_inc(S(name), 1)

            def piece(name, rec, post):
                if name == "xt":
                    pe.wait_ge(S("xn_done"), B)
                    to_channels(bank[4], xn, "xt_mm")
                if name == "route":
                    pe.wait_ge(S("xnc_done"), 1)
                    if post:
                        pe.wait_ge(S("o_read"), 1)
                    for g in range(B):
                        for c in range(2):
                            last = mm(bank[5][:, g * 136:(g + 1) * 136], xnc[:, c, g, 1:L + 1], w["route"][:, c, :],
                                      start=(c == 0), stop=(c == 1))
                    last.then_inc(S("route_mm"), 1)
                if name == "mix":
                    pe.wait_ge(S("xm_done"), 2)
                    if rec:
                        pe.wait_ge(S("y1_read"), 1)
                    for u, m in ((0, 128), (1, 64)):
                        for c in range(2):
                            last = mm(bank[7][0:m, u * 256:(u + 1) * 256], w["x_A"][:, c, u * 128:u * 128 + m], xm[:, c, :],
                                      start=(c == 0), stop=(c == 1))
                    last.then_inc(S("mix_mm"), 1)
                if name.startswith("miu"):
                    ks = [int(k) for k in name[3:]]
                    if ks[0] == 0:
                        pe.wait_ge(S("mixt_done"), 2)
                        if post:
                            pe.wait_ge(S("zt_done"), 1)
                    else:
                        pe.wait_ge(S("miu_read"), 2 * ks[0])
                    for c in range(2):
                        for k in ks:
                            q = MIX_ORDER[k]
                            o, u = 32 * (q % 4), q // 4
                            last = mm(bank[4 + 2 * (k % 2)][:, c * 256:(c + 1) * 256],
                                      w["x_B"][o:o + 32, u, c * 128:(c + 1) * 128], mixt[o:o + 32, u, :], start=True, stop=True)
                    last.then_inc(S("miu_mm"), 1)
                if name == "xmt":
                    pe.wait_ge(S("agate_done"), 2)
                    pe.wait_ge(S("xmask_done"), 2)
                    for j in range(2):
                        for g in range(B):
                            last = tr(bank[7][:, (j * B + g) * L:(j * B + g + 1) * L], xmask[:, j, g, :], ident[:])
                    last.then_inc(S("xmt_mm"), 1)
                if name == "w_A":
                    pe.wait_ge(S("mixt_done"), 2)
                    low(bank[7], "w_A", W_, 64)
                if name == "k_A":
                    pe.wait_ge(S("route_read"), 1)
                    low(bank[5], "k_A", K_, 64)
                if name == "a_A":
                    pe.wait_ge(S("hw_done"), 1)
                    low(bank[7], "a_A", A_, 64)
                if name == "w_B":
                    pe.wait_ge(S("hk_done"), 1)
                    for c in range(2):
                        last = mm(bank[5][:, c * 256:(c + 1) * 256], w["w_B"][0:64, c * 128:(c + 1) * 128], h_w[:],
                                  start=True, stop=True)
                    last.then_inc(S("w_B_mm"), 1)
                if name == "kW":
                    pe.wait_ge(S("miu_read"), 10)
                    for c in range(2):
                        for k in range(2):
                            mm(bank[4][:, c * 256:(c + 1) * 256], w["kW"][:, k, c * 128:(c + 1) * 128], xd[:, K_, k, :],
                               start=(c == 0 and k == 0), stop=False, skip_group_check=True)
                if name == "r":
                    pe.wait_ge(S("xd_done"), SLOT[R_] + 1)
                    pe.wait_ge(S("miu_read"), 12)
                    for c in range(2):
                        for k in range(2):
                            last = mm(bank[6][:, c * 256:(c + 1) * 256], w["rW"][:, k, c * 128:(c + 1) * 128],
                                      xd[:, R_, k, :], start=(k == 0), stop=(k == 1))
                    last.then_inc(S("r_mm"), 1)
                if name == "a_B":
                    pe.wait_ge(S("ha_done"), 1)
                    for c in range(2):
                        last = mm(bank[7][:, c * 256:(c + 1) * 256], w["a_B"][0:64, c * 128:(c + 1) * 128], h_a[:],
                                  start=True, stop=True)
                    last.then_inc(S("a_B_mm"), 1)
                if name == "k_B":
                    pe.wait_ge(S("hk_done"), 1)
                    for c in range(2):
                        last = mm(bank[4][:, c * 256:(c + 1) * 256], w["k_B"][0:64, c * 128:(c + 1) * 128], h_k[:],
                                  start=False, stop=True, skip_group_check=True)
                    last.then_inc(S("k_mm"), 1)
                if name == "v":
                    pe.wait_ge(S("xd_done"), SLOT[V_] + 1)
                    pe.wait_ge(S("sig_done"), 2)
                    for g in range(B):
                        for k in range(2):
                            last = mm(bank[5][:, g * C:(g + 1) * C], xd[:, V_, k, g * L:(g + 1) * L], w["vW"][:, k, :],
                                      start=(k == 0), stop=(k == 1))
                    last.then_inc(S("v_mm"), 1)
                if name == "g_A":
                    pe.wait_ge(S("r_done"), 1)
                    low(bank[6], "g_A", G_, 128)
                if name == "norm":
                    pe.wait_ge(S("ksum_done"), 1)
                    mm(DB[:, 0:B * L], ones[:], ksum[:], start=True, stop=True).then_inc(S("nrm_mm"), 1)
                if name == "g_B":
                    pe.wait_ge(S("hg_done"), 1)
                    pe.wait_ge(S("xmt_done"), 1)
                    for g in range(B):
                        last = mm(bank[7][:, g * C:(g + 1) * C], h_g[:, g * L:(g + 1) * L], w["g_B"][:], start=True, stop=True)
                    last.then_inc(S("gate_mm"), 1)
                if name == "zt":
                    to_channels(bank[6], zz, "zt_mm")
                if name == "o":
                    pe.wait_ge(S("zt_done"), 1)
                    for g in range(B):
                        for c in range(2):
                            last = mm(bank[5][:, g * C:(g + 1) * C], zt[:, c, g, :], w["oW"][:, c, :],
                                      start=(c == 0), stop=(c == 1))
                    last.then_inc(S("o_mm"), 1)

            def gram(l, g):
                n, m = 2 * l + g, 1 << l
                if l:
                    pe.wait_ge(S("ar_scaled"), 2 * (l - 1) + g + 1)
                if 1 <= l < PACKED:
                    pe.wait_ge(S("bk_scaled"), 2 * (l - 1) + g + 1)
                if l >= PACKED:
                    pe.wait_ge(S("bk_packed"), 4 * (l - PACKED) + 2 * g + 2)
                if n:
                    pe.wait_ge(S("g0_stored"), n)
                    pe.wait_ge(S("g1_stored"), n)
                for kind in range(2 if l < PACKED else 1):
                    for c in range(2):
                        for p in range(2):
                            o = 64 * p
                            rhs = ar[o:o + 64, g, :, c, :].rearrange("p a (n two m) -> p a n two m", two=2, m=m)[:, :, :, 1, :]
                            keys = bk[o:o + 64, g, kind, c, :] if l < PACKED else \
                                bkp[o:o + 64, g, c, :, :].rearrange("p k n -> p (k n)")
                            last = mm(GB[p][:, (2 * kind + c) * 128:(2 * kind + c + 1) * 128], keys, rhs, start=True, stop=True)
                last.then_inc(S("g_mm"), 1)

            def inv_x(l, g):
                pe.wait_ge(S("tr_done"), 2 * (l - 1) + g + 1)
                pe.wait_ge(S("g0_stored"), 2 * l + g + 1)
                pe.wait_ge(S("g1_stored"), 2 * l + g + 1)
                for h in range(H):
                    last = mm(CB[g][:, h * HALF:(h + 1) * HALF], gm[:, g, h // 2, 0, h % 2, 0, :],
                              left(tinv[:, g, h, :], 1 << l), start=True, stop=True)
                last.then_inc(S("x_mm"), 1)

            def inv_off(l, g):
                pe.wait_ge(S("x_done"), 2 * (l - 1) + g + 1)
                for h in range(H):
                    last = mm(CB[g][:, 256 + h * HALF:256 + (h + 1) * HALF], tinvT[:, g, h, :], xb[:, g, h, :],
                              start=True, stop=True)
                last.then_inc(S("off_mm"), 1)

            def inv_tr(l, g):
                if l == 0:
                    pe.wait_ge(S("inv1_done"), 2 * g + 2)
                else:
                    pe.wait_ge(S("inv_added"), 2 * (l - 1) + g + 1)
                for h in range(H):
                    last = tr(CB[g][:, h * L:(h + 1) * L], (tinvT if l == 0 else tinv)[:, g, h, :], ident[:])
                last.then_inc(S("tr_mm"), 1)

            def top_x(g):
                pe.wait_ge(S("tr_done"), 2 * (TOP - 1) + g + 1)
                pe.wait_ge(S("g0_stored"), 2 * TOP + g + 1)
                pe.wait_ge(S("g1_stored"), 2 * TOP + g + 1)
                for h in range(H):
                    last = mm(CB[g][HALF:L, h * HALF:(h + 1) * HALF], gm[:, g, h // 2, 0, h % 2, 0, HALF:L],
                              tinv[:, g, h, 0:HALF], start=True, stop=True)
                last.then_inc(S("x_mm"), 1)

            def top_off(g):
                pe.wait_ge(S("x_done"), 2 * (TOP - 1) + g + 1)
                for h in range(H):
                    last = mm(CB[g][0:HALF, 256 + h * HALF:256 + (h + 1) * HALF], xb[HALF:L, g, h, :],
                              tinvT[HALF:L, g, h, HALF:L], start=True, stop=True)
                last.then_inc(S("off_mm"), 1)

            def keys_to_tokens(g):
                pe.wait_ge(S("bk_scaled"), 2 * TOP + g + 1)
                if g:
                    pe.wait_ge(S("bkt_done"), g)
                for j in range(2):
                    for c in range(2):
                        last = tr(DB[:, (j * 2 + c) * L:(j * 2 + c + 1) * L], bk[:, g, j, c, :], ident[:])
                last.then_inc(S("bkt_mm"), 1)

            def tile(step, front, rec, post):
                def pieces(names):
                    for name in names:
                        if post if name in POST else front:
                            piece(name, rec, post)

                def feed(todo):
                    if front:
                        for kind, p in todo:
                            ffn(kind, p, rec)

                pe.wait_ge(go, step)
                if rec:
                    ffn(*LATE[0], rec)
                else:
                    mm(bank[6][:, 0:128], ident[:], ident[:], start=True, stop=True)
                for l in range(LEVELS):
                    if l == 3 and not rec:
                        wait_loaded(pe, 1)
                    pieces(BEFORE[l])
                    if rec:
                        if l >= 2:
                            inv_x(l - 1, 0)
                        gram(l, 0)
                        if l == 0:
                            ffn(*LATE[1], rec)
                        if l == 1:
                            inv_tr(0, 0)
                            inv_tr(0, 1)
                        if l >= 2:
                            inv_x(l - 1, 1)
                            inv_off(l - 1, 0)
                    pieces(BETWEEN[l])
                    if rec:
                        gram(l, 1)
                        if l >= 2:
                            inv_off(l - 1, 1)
                            inv_tr(l - 1, 0)
                    pieces(AFTER[l])
                    if rec and l >= 2:
                        inv_tr(l - 1, 1)
                pieces(["norm"])
                if rec:
                    top_x(0)
                    top_x(1)
                pieces(["g_B"])
                if not rec:
                    wait_loaded(pe, 2)
                    pe.wait_ge(zeroed_late, len(ZEROED_LATE))
                if rec:
                    for g in range(B):
                        pe.wait_ge(S("ar_scaled"), 2 * TOP + g + 1)
                        pe.wait_ge(S("g0_stored"), 2 * LEVELS)
                        pe.wait_ge(S("g1_stored"), 2 * LEVELS)
                        if g == 0:
                            pe.wait_ge(S("vr_done"), 1)
                        for c in range(2):
                            mm(GB[g][:, c * 128:(c + 1) * 128], ar[:, g, 0, c, :], state[:, g, c, :], start=True, stop=False,
                               skip_group_check=True)
                            for h in (2 * c, 2 * c + 1):
                                last = mm(GB[g][:, h * N:(h + 1) * N], gm[:, g, h % 2, 1, c, 0, :],
                                          v_r[:, g, h * N:(h + 1) * N], start=False, stop=True, skip_group_check=True)
                        last.then_inc(S("p_mm"), 1)
                    top_off(0)
                    top_off(1)
                feed(FFN_INV)
                if rec:
                    if front:
                        pe.wait_ge(S("nrm_done"), 1)
                    keys_to_tokens(0)
                feed(FFN_TR)
                if rec:
                    keys_to_tokens(1)
                    for g in range(B):
                        pe.wait_ge(S("inv_finished"), g + 1)
                        pe.wait_ge(S("p_done"), g + 1)
                        for h in range(H):
                            last = mm(GB[g][:, 256 + h * N:256 + (h + 1) * N], tinvT[:, g, slot(h), :], pp[:, g, h, :],
                                      start=True, stop=True)
                        last.then_inc(S("sa_mm"), 1)
                feed(FFN_SA)
                if rec:
                    for g in range(B):
                        pe.wait_ge(S("sa_done"), g + 1)
                        for c in range(2):
                            mm(CB[g][:, c * 128:(c + 1) * 128], ar[:, g, 1, c, :], state[:, g, c, :], start=True, stop=False,
                               skip_group_check=True)
                            for h in (2 * c, 2 * c + 1):
                                dst = CB[g][:, h * N:(h + 1) * N]
                                mm(dst, gm[:, g, h % 2, 0, c, 1, :], sa[:, g, h, :], start=False, stop=False,
                                   skip_group_check=True)
                                last = mm(dst, gm[:, g, h % 2, 1, c, 1, :], v_r[:, g, h * N:(h + 1) * N], start=False,
                                          stop=True, skip_group_check=True)
                        last.then_inc(S("y_mm"), 1)
                        pe.wait_ge(S("bkt_done"), g + 1)
                        for c in range(2):
                            dst = GB[g][:, c * 128:(c + 1) * 128]
                            mm(dst, bkt[:, g, 0, c, :], sa[:, g, 2 * c:2 * c + 2, :], start=True, stop=False)
                            last = mm(dst, bkt[:, g, 1, c, :], v_r[:, g, c * 128:(c + 1) * 128], start=False, stop=True)
                        last.then_inc(S("inc_mm"), 1)
                feed(FFN_Y)

            wait_loaded(pe, 0)
            pe.wait_ge(zeroed, NZ)
            tile(1, True, False, False)
            with pe.Fori(0, TILES - 1) as i:
                tile(i + 2, True, True, True)
            tile(TILES + 1, False, True, True)
            tile(TILES + 2, False, False, True)

        @block.scalar
        def _(act):
            A = nc.scalar.activation

            def relu(which, p):
                act.wait_ge(S(f"z{which}_mm"), p + 1)
                if p >= 2:
                    act.wait_ge(S("hid_done"), p - 1)
                dst = relu1 if which == 1 else relu2
                for j in range(2):
                    A(dst[:, p % 2, j * 256:(j + 1) * 256], ZB[p % 2][:, j * 256:(j + 1) * 256], ACT.Relu,
                      bias=prm[:, P_BI + 2 * p + j:P_BI + 2 * p + j + 1]).then_inc(S(f"relu{which}_done"), 1)

            def inv_tr(l, g):
                act.wait_ge(S("tr_mm"), 2 * l + g + 1)
                dst = tinv if l == 0 else tinvT
                A(dst[:, g, :, :], CB[g][:, :], ACT.Copy).then_inc(S("tr_done"), 1)

            def pack_bk(l, g):
                act.wait_ge(S("bk_scaled"), 2 * (l - 1) + g + 1)
                for kind in range(2):
                    A(bkp[:, g, :, kind, :].rearrange("p c (n m) -> p c n m", m=1 << l),
                      bk[:, g, kind, :, :].rearrange("p c (n two m) -> p c n two m", two=2, m=1 << l)[:, :, :, 0, :],
                      ACT.Copy).then_inc(S("bk_packed"), 1)

            def biased_sigmoid(dst, src, col, name):
                for c in range(2):
                    A(dst[:, :, c, :], src[:, c * 256:(c + 1) * 256].rearrange("p (g t) -> p g t", g=B), ACT.Sigmoid,
                      bias=prm[:, col + c:col + c + 1]).then_inc(S(name), 1)

            def piece(name, rec):
                if name == "xt":
                    act.wait_ge(S("xt_mm"), 1)
                    act.wait_ge(S("carry_done"), 1)
                    A(xnc[:, :, :, 1:L + 1], bank[4][:, :].rearrange("p (c g t) -> p c g t", c=2, g=B), ACT.Copy)\
                        .then_inc(S("xnc_done"), 1)
                if name == "route":
                    act.wait_ge(S("route_mm"), 1)
                    A(rt[:, :, :], bank[5][:, 0:272], ACT.Copy).then_inc(S("route_read"), 1)
                if name == "mix":
                    act.wait_ge(S("mix_mm"), 1)
                    A(mixt[:, 0, :], bank[7][:, 0:256], ACT.Tanh).then_inc(S("mixt_done"), 1)
                    A(mixt[0:64, 1, :], bank[7][0:64, 256:512], ACT.Tanh).then_inc(S("mixt_done"), 1)
                if name == "xmt":
                    act.wait_ge(S("xmt_mm"), 1)
                    A(xmt[:, :, :], bank[7][:, :], ACT.Copy).then_inc(S("xmt_done"), 1)
                if name == "w_A":
                    act.wait_ge(S("w_A_mm"), 1)
                    A(h_w[:], bank[7][0:64, 0:256], ACT.Tanh).then_inc(S("hw_done"), 1)
                if name == "k_A":
                    act.wait_ge(S("k_A_mm"), 1)
                    A(h_k[:], bank[5][0:64, 0:256], ACT.Tanh).then_inc(S("hk_done"), 1)
                    act.wait_ge(S("nm1_done"), 1)
                    for g in range(B):
                        A(e8[:, g, :], lg[:, g, :], ACT.Exp, bias=nm1[:, g:g + 1]).then_inc(S("e8_done"), 1)
                        A(e2[:, g:g + 1], top8[:, g, 1:2], ACT.Exp, bias=nm1[:, g:g + 1]).then_inc(S("e8_done"), 1)
                if name == "a_A":
                    act.wait_ge(S("a_A_mm"), 1)
                    A(h_a[:], bank[7][0:64, 0:256], ACT.Copy).then_inc(S("ha_done"), 1)
                if name == "w_B":
                    act.wait_ge(S("w_B_mm"), 1)
                    biased_sigmoid(sig, bank[5], P_WMIU, "sig_done")
                if name == "r":
                    act.wait_ge(S("r_mm"), 1)
                    A(rr[:, :, :, :], gct(bank[6][:, :]), ACT.Copy).then_inc(S("r_done"), 1)
                if name == "a_B":
                    act.wait_ge(S("a_B_mm"), 1)
                    biased_sigmoid(agate, bank[7], P_ATIME, "agate_done")
                if name == "k_B":
                    act.wait_ge(S("k_mm"), 1)
                    A(kraw[:, :, :, :], gct(bank[4][:, :]), ACT.Copy).then_inc(S("kraw_done"), 1)
                    A(ksq[:, :, :], bank[4][:, :], ACT.Square).then_inc(S("ksq_done"), 1)
                if name == "v":
                    act.wait_ge(S("v_mm"), 1)
                    if rec:
                        act.wait_ge(S("vr_done"), 1)
                    A(vt[:, :, :], bank[5][:, :], ACT.Copy).then_inc(S("v_done"), 1)
                if name == "g_A":
                    act.wait_ge(S("g_A_mm"), 1)
                    A(h_g[:], bank[6][:, 0:256], ACT.Tanh).then_inc(S("hg_done"), 1)
                if name == "norm":
                    act.wait_ge(S("nrm_mm"), 1)
                    A(nrm[:, :, :], DB[:, 0:256], ACT.Sqrt).then_inc(S("nrm_done"), 1)
                    act.wait_ge(S("sig_done"), 2)
                    A(rootd[:, :, :, :], sig[:, :, :, :], ACT.Sqrt, scale=math.exp(-0.5)).then_inc(S("rootd_done"), 1)
                if name == "g_B":
                    act.wait_ge(S("gate_mm"), 1)
                    if rec:
                        act.wait_ge(S("gate_moved"), 1)
                    A(gate[:, :, :], bank[7][:, :], ACT.Copy).then_inc(S("gate_done"), 1)
                if name == "zt":
                    act.wait_ge(S("zt_mm"), 1)
                    A(zt[:, :, :, :], bank[6][:, :], ACT.Copy).then_inc(S("zt_done"), 1)

            def tile(step, front, rec, post):
                def pieces(names):
                    for name in names:
                        if post if name in POST else front:
                            piece(name, rec)

                def feed(todo):
                    if front:
                        for kind, p in todo:
                            if kind == "lora":
                                relu(1, p)
                            if kind == "diff":
                                relu(2, p)

                act.wait_ge(go, step)
                A(scratch[:, 0:1], eps[:, 0:1], ACT.Copy)
                if front:
                    act.wait_ge(S("var_done"), B)
                    A(rstd[:, :], mv[:, :, 1], ACT.Sqrt, bias=eps[:, 0:1]).then_inc(S("std_done"), 1)
                if rec:
                    A(v_r[:, :, :], vt[:, :, :], ACT.Copy).then_inc(S("vr_done"), 1)
                for l in range(LEVELS):
                    pieces(BEFORE[l])
                    if rec and l == 1:
                        inv_tr(0, 0)
                        inv_tr(0, 1)
                    pieces(BETWEEN[l])
                    if rec and PACKED - 1 <= l < TOP:
                        pack_bk(l + 1, 0)
                    if rec and l >= 2:
                        inv_tr(l - 1, 0)
                    pieces(AFTER[l])
                    if rec and l >= 2:
                        inv_tr(l - 1, 1)
                    if rec and PACKED - 1 <= l < TOP:
                        pack_bk(l + 1, 1)
                    if l == 4 and rec:
                        if post:
                            act.wait_ge(S("out_done"), 1)
                        A(gate_r[:, :, :], gate[:, :, :], ACT.Copy).then_inc(S("gate_moved"), 1)
                        A(x_b[:, :, :], x_a[:, :, :], ACT.Copy).then_inc(S("xb_moved"), 1)
                    if l == 4 and front:
                        if rec:
                            act.wait_ge(S("xb_moved"), 1)
                        A(x_a[:, :, :], x_in[:, :, :], ACT.Copy).then_inc(S("xa_moved"), 1)
                    if l == 5 and rec:
                        act.wait_ge(S("ypre_done"), B)
                        A(ysg[:, :, :], y1[:, :, :], ACT.Sigmoid).then_inc(S("ysg_done"), 1)
                pieces(["norm", "g_B"])
                if rec:
                    for g in range(B):
                        act.wait_ge(S("p_mm"), g + 1)
                        A(pp[:, g, :, :], GB[g][:, 0:256], ACT.Copy).then_inc(S("p_done"), 1)
                feed(FFN_INV)
                if rec:
                    act.wait_ge(S("bkt_mm"), 1)
                    A(bkt[:, 0, :, :, :], DB[:, :], ACT.Copy).then_inc(S("bkt_done"), 1)
                feed(FFN_TR)
                if rec:
                    act.wait_ge(S("bkt_mm"), 2)
                    A(bkt[:, 1, :, :, :], DB[:, :], ACT.Copy).then_inc(S("bkt_done"), 1)
                    for g in range(B):
                        act.wait_ge(S("sa_mm"), g + 1)
                        A(sa[:, g, :, :], GB[g][:, 256:512], ACT.Copy).then_inc(S("sa_done"), 1)
                feed(FFN_SA)
                if rec:
                    for g in range(B):
                        act.wait_ge(S("y_mm"), g + 1)
                        A(yy[:, g, :, :], CB[g][:, 0:256], ACT.Copy).then_inc(S("y_done"), 1)
                if front:
                    if rec:
                        act.wait_ge(S("y_mm"), B)
                    act.wait_ge(S("kh_done"), 1)
                    A(ar[:, :, 0, :, :], kh[:, :, :, :], ACT.Copy, scale=-1.0).then_inc(S("ar0_ready"), 1)
                    for g in range(B):
                        A(tinvT[:, g, :, :], ident[:].unsqueeze(1).to_broadcast([128, H, L]), ACT.Copy)\
                            .then_inc(S("inv0_done"), 1)
                feed(FFN_Y[:2])
                if rec:
                    act.wait_ge(S("yc_done"), 1)
                    A(ysq[:, :, :], yc[:, :, :], ACT.Square).then_inc(S("ysq_done"), 1)
                feed(FFN_Y[2:5])
                if rec:
                    act.wait_ge(S("v8_done"), 1)
                    A(sd8[:], v8[:], ACT.Sqrt, scale=1.0 / N, bias=eps[:, 1:2]).then_inc(S("sd8_done"), 1)
                feed(FFN_Y[5:])
                A(scratch[:, 1:2], eps[:, 0:1], ACT.Copy).then_inc(S("act_end"), 1)

            wait_loaded(act, 0)
            act.wait_ge(zeroed, NZ)
            tile(1, True, False, False)
            with act.Fori(0, TILES - 1) as i:
                tile(i + 2, True, True, True)
            tile(TILES + 1, False, True, True)
            tile(TILES + 2, False, False, True)

        @block.gpsimd
        def _(pool):
            tt = nc.gpsimd.tensor_tensor

            def mixed(k, rec):
                q = MIX_ORDER[k]
                pool.wait_ge(S("miu_read"), 2 * k + 2)
                if k == 0 and rec:
                    pool.wait_ge(S("down_late_mm"), 2)
                tt(xd[:, q, :, :], mtmp[:, k % 2, :, :].rearrange("p c (g t) -> p c g t", g=B),
                   xnc[:, :, :, 1:L + 1], ALU.add).then_inc(S("xd_done"), 1)

            def scale_bk(l, g):
                m, n = 1 << l, HALF >> l
                tv = tot[l][:, g, :, :].rearrange("p c (n two) -> p (c n) two", two=2)
                if l:
                    pool.wait_ge(S("tot_done"), 2 * (l - 1) + g + 1)
                tt(tot[l + 1][:, g, :, :].rearrange("p c n -> p (c n)"), tv[:, :, 0], tv[:, :, 1], ALU.mult)\
                    .then_inc(S("tot_done"), 1)
                pool.wait_ge(S("g_mm"), 2 * l + g + 1)
                if l:
                    pool.wait_ge(S("bk_scaled"), 2 * (l - 1) + g + 1)
                v = bk[:, g, :, :, :].rearrange("p a c (n two m) -> p a (c n) two m", two=2, m=m)[:, :, :, 0, :]
                tt(v, v, tv[:, :, 1].unsqueeze(1).unsqueeze(3).to_broadcast([128, 2, 2 * n, m]), ALU.mult)\
                    .then_inc(S("bk_scaled"), 1)

            def tile(step, front, rec, post):
                def pieces(names):
                    for name in names:
                        if front and name.startswith("miu"):
                            for k in name[3:]:
                                mixed(int(k), rec)

                pool.wait_ge(go, step)
                tt(scratchp[:, 0:1], eps[:, 0:1], eps[:, 0:1], ALU.add)
                for l in range(LEVELS):
                    pieces(BEFORE[l])
                    if rec:
                        scale_bk(l, 0)
                        scale_bk(l, 1)
                    if l == 1 and post:
                        pool.wait_ge(S("o_read"), 1)
                        tt(out_t[:, :, :], out_t[:, :, :], x_b[:, :, :], ALU.add).then_inc(S("out_done"), 1)
                    if l == 4 and rec:
                        pool.wait_ge(S("vr_done"), 1)
                        tt(bv[:, :, :, :], v_r[:, :, :].rearrange("p g (h n) -> p g h n", n=N),
                           bonus[:, :, :].unsqueeze(3).to_broadcast([128, B, H, N]), ALU.mult).then_inc(S("bv_done"), 1)
                        pool.wait_ge(S("bv_done"), 1)
                        tt(bv[:, :, :, :].rearrange("p g h n -> p g (h n)"), bv[:, :, :, :].rearrange("p g h n -> p g (h n)"),
                           w["beta"][:].unsqueeze(1).to_broadcast([128, B, C]), ALU.add).then_inc(S("bv_shifted"), 1)
                    pieces(AFTER[l])
                if front:
                    pool.wait_ge(S("ksq_done"), 1)
                    tt(ksum[:], ksq[:, 0, :], ksq[:, 1, :], ALU.add).then_inc(S("ksum_done"), 1)
                    pool.wait_ge(S("kh_done"), 1)
                    pool.wait_ge(S("rootd_done"), 1)
                    if rec:
                        pool.wait_ge(S("bkt_mm"), B)
                    tt(bk[:, :, 1, :, :], kh[:, :, :, :], rootd[:, :, :, :], ALU.mult).then_inc(S("bk1_ready"), 1)
                    pool.wait_ge(S("bk1_ready"), 1)
                    pool.wait_ge(S("r_done"), 1)
                    tt(dg[:, 1, :, :, :], rr[:, :, :, :], bk[:, :, 1, :, :], ALU.mult).then_inc(S("dg_done"), 1)
                    pool.wait_ge(S("bk0_ready"), 1)
                    tt(dg[:, 0, :, :, :], rr[:, :, :, :], bk[:, :, 0, :, :], ALU.mult).then_inc(S("dg_done"), 1)
                tt(scratchp[:, 1:2], eps[:, 0:1], eps[:, 0:1], ALU.add).then_inc(S("pool_end"), 1)

            for buf in ZEROED_LATE:
                nc.gpsimd.memset(buf[:], 0.0).then_inc(zeroed_late, 1)
            pool.wait_ge(zeroed, NZ)
            tile(1, True, False, False)
            with pool.Fori(0, TILES - 1) as i:
                tile(i + 2, True, True, True)
            tile(TILES + 1, False, True, True)
            tile(TILES + 2, False, False, True)

        @block.vector
        def _(dve):
            v = nc.vector
            count = {}

            def run(ins, name="dve_step"):
                count[name] = count.get(name, 0) + 1
                ins.then_inc(S(name), 1)
                return name, count[name]

            def need(token):
                dve.wait_ge(S(token[0]), token[1])

            def store(l, g, p):
                m = 1 << l
                n = HALF // m
                dve.wait_ge(S("g_mm"), 2 * l + g + 1)
                if l:
                    dve.wait_ge(S(f"g{p}_stored"), 2 * (l - 1) + g + 1)
                if l >= PACKED:
                    for kind in range(2):
                        for i in range(n):
                            src = GB[p][HALF * kind + m * i:HALF * kind + m * (i + 1), 0:256]
                            ins = v.tensor_copy(gm[2 * m * i:2 * m * i + m, g, p, kind, :, :, 2 * m * i + m:2 * m * (i + 1)]
                                                .rearrange("p c a t -> p (c a) t"),
                                                src.rearrange("p (x n m) -> p x n m", x=4, m=m)[:, :, i, :])
                    run(ins, f"g{p}_stored")
                    return
                src = GB[p][:, :].rearrange("p (x n m) -> p x n m", x=8, m=m)
                dst = gm[:, g, p].rearrange("p k c a (n two m) -> p (k c a) n two m", two=2, m=m)[:, :, :, 1, :]
                msk = mask_g[:, l, :].rearrange("p (n m) -> p n m", m=m).unsqueeze(1)
                run(v.copy_predicated(dst, msk.to_broadcast([128, 8, n, m]), src), f"g{p}_stored")

            def start_inverse(g):
                for p in range(2):
                    dve.wait_ge(S(f"g{p}_stored"), g + 1)
                    run(v.copy_predicated(tinvT[:, g, 2 * p:2 * p + 2, :].rearrange("p h (n two) -> p h n two", two=2)[:, :, :, 1],
                                          mask_g[:, 0, :].unsqueeze(1).to_broadcast([128, 2, HALF]),
                                          gm[:, g, p, 0, :, 0, :].rearrange("p h (n two) -> p h n two", two=2)[:, :, :, 1]),
                        "inv1_done")

            def scale_ar(l, g):
                m, n = 1 << l, HALF >> l
                dve.wait_ge(S("g_mm"), 2 * l + g + 1)
                if l:
                    dve.wait_ge(S("tot_done"), 2 * (l - 1) + g + 1)
                    dve.wait_ge(S("ar_scaled"), 2 * (l - 1) + g + 1)
                tv = tot[l][:, g, :, :].rearrange("p c (n two) -> p (c n) two", two=2)
                a = ar[:, g, :, :, :].rearrange("p a c (n two m) -> p a (c n) two m", two=2, m=m)[:, :, :, 1, :]
                run(v.tensor_tensor(a, a, tv[:, :, 0].unsqueeze(1).unsqueeze(3).to_broadcast([128, 2, 2 * n, m]),
                                    ALU.mult), "ar_scaled")

            def keep_x(l, g):
                dve.wait_ge(S("x_mm"), 2 * (l - 1) + g + 1)
                run(v.tensor_tensor(xb[:, g, :, :], CB[g][:, 0:256].rearrange("p (h n) -> p h n", h=H),
                                    mask_x[:, l, :].unsqueeze(1).to_broadcast([128, H, HALF]), ALU.mult), "x_done")

            def add_off(l, g):
                m = 1 << l
                dve.wait_ge(S("off_mm"), 2 * (l - 1) + g + 1)
                tl = tinv[:, g, :, :].rearrange("p h (n two m) -> p (h n) two m", two=2, m=m)[:, :, 0, :]
                run(v.tensor_tensor(tl, tl, CB[g][:, 256:512].rearrange("p (n m) -> p n m", m=m), ALU.add), "inv_added")

            def router(stage):
                if stage == 0:
                    dve.wait_ge(S("route_read"), 1)
                    need(run(v.tensor_tensor(lg[:, :, :], rt[:, :, 128:136],
                                             w["gate_b"][:].unsqueeze(1).to_broadcast([128, B, E]), ALU.add)))
                    t = [run(v.max(top8[:, g, :], lg[:, g, :])) for g in range(B)][-1]
                    need(t)
                    run(v.tensor_scalar(nm1[:, :], top8[:, :, 0], -1.0, None, ALU.mult), "nm1_done")
                    for g in range(B):
                        t = run(v.scalar_tensor_tensor(hit[:, g, :], lg[:, g, :], top8[:, g, 0:1], rev8[:],
                                                       ALU.is_ge, ALU.mult))
                    need(t)
                    need(run(v.tensor_reduce(hmx[:, :], hit[:, :, :], AX.X, ALU.max)))
                    for g in range(B):
                        run(v.tensor_scalar(oh1[:, g, :], hit[:, g, :], hmx[:, g:g + 1], None, ALU.is_equal), "oh1_done")
                if stage == 1:
                    need(("oh1_done", B))
                    need(run(v.tensor_scalar(rest[:, :, :], oh1[:, :, :], -1.0, 1.0, ALU.mult, ALU.add)))
                    for g in range(B):
                        t = run(v.scalar_tensor_tensor(hit[:, g, :], lg[:, g, :], top8[:, g, 1:2], rest[:, g, :],
                                                       ALU.is_ge, ALU.mult))
                    need(t)
                    need(run(v.tensor_tensor(hit[:, :, :], hit[:, :, :], rev8[:].unsqueeze(1).to_broadcast([128, B, E]),
                                             ALU.mult)))
                    need(run(v.tensor_reduce(hmx[:, :], hit[:, :, :], AX.X, ALU.max)))
                    for g in range(B):
                        run(v.tensor_scalar(oh2[:, g, :], hit[:, g, :], hmx[:, g:g + 1], None, ALU.is_equal), "oh2_done")
                if stage == 2:
                    need(("oh2_done", B))
                    need(run(v.tensor_tensor(oh2[:, :, :], oh2[:, :, :], oh1[:, :, :], ALU.subtract)))
                    for j, o in enumerate((oh1, oh2)):
                        run(v.tensor_tensor(xmask[:, j, :, :].rearrange("p g (e r) -> p g e r", r=RANK),
                                            rt[:, :, 0:128].rearrange("p g (e r) -> p g e r", r=RANK),
                                            o[:, :, :].unsqueeze(3).to_broadcast([128, B, E, RANK]), ALU.mult), "xmask_done")

            def hidden(p):
                dve.wait_ge(S("relu1_done"), 2 * p + 2)
                dve.wait_ge(S("relu2_done"), 2 * p + 2)
                if p == 0:
                    dve.wait_ge(S("g_A_mm"), 1)
                run(v.tensor_tensor(hid[:, p, :], relu1[:, p % 2, :], relu2[:, p % 2, :], ALU.add), "hid_done")

            def gate_sum():
                dve.wait_ge(S("e8_done"), 2 * B)
                need(run(v.tensor_reduce(esum[:, :], e8[:, :, :], AX.X, ALU.add)))
                need(run(v.reciprocal(esum[:, :], esum[:, :])))
                need(run(v.scalar_tensor_tensor(vsum[:, :], e2[:, :], 1.0, esum[:, :], ALU.add, ALU.mult)))

            def mixed(k):
                q = MIX_ORDER[k]
                dve.wait_ge(S("miu_mm"), k // 2 + 1)
                if k >= 2:
                    dve.wait_ge(S("xd_done"), k - 1)
                for c in range(2):
                    run(v.scalar_tensor_tensor(mtmp[:, k % 2, c, :], bank[4 + 2 * (k % 2)][:, c * 256:(c + 1) * 256],
                                               prm[:, P_LAM + 2 * q + c:P_LAM + 2 * q + c + 1], dx[:, c, :],
                                               ALU.add, ALU.mult), "miu_read")

            yv = yy[:, :, :, :].rearrange("p g h n -> p (g h) n")

            def tile(step, front, rec, post):
                count.clear()

                def pieces(names):
                    for name in names:
                        if name.startswith("miu") and front:
                            for k in name[3:]:
                                mixed(int(k))
                        if name == "o" and post:
                            dve.wait_ge(S("o_mm"), 1)
                            run(v.tensor_tensor(out_t[:, :, :], bank[5][:, :].rearrange("p (g n) -> p g n", g=B),
                                                     fgate[:, :, :], ALU.mult), "o_read")

                dve.wait_ge(go, step)
                v.memset(scratch[:, 2:3], 0.0)
                if front:
                    for g in range(B):
                        need(run(v.bn_stats(st6[:, g, :], x_in[:, g, :])))
                        run(v.bn_aggr(mv[:, g, :], st6[:, g, :]), "var_done")
                    carried = run(v.tensor_copy(xnc[:, :, :, 0], xnc[:, :, :, L]), "carry_done")
                for l in range(LEVELS):
                    pieces(BEFORE[l])
                    if rec:
                        if l >= 2:
                            keep_x(l - 1, 0)
                        store(l, 0, 0)
                        store(l, 0, 1)
                        scale_ar(l, 0)
                        if l == 0:
                            start_inverse(0)
                        if l >= 2:
                            keep_x(l - 1, 1)
                            add_off(l - 1, 0)
                    if l == 0 and front:
                        dve.wait_ge(S("std_done"), 1)
                        need(run(v.reciprocal(rstd[:, :], rstd[:, :])))
                        for g in range(B):
                            run(v.tensor_scalar(xn[:, g, :], x_in[:, g, :], mv[:, g, 0:1], rstd[:, g:g + 1],
                                                ALU.subtract, ALU.mult), "xn_done")
                    if l == 2 and rec:
                        dve.wait_ge(S("down_late_mm"), 2)
                        run(v.scalar_tensor_tensor(y1[:, :, :], w["bo"][:].unsqueeze(1).to_broadcast([128, B, C]), 2.0,
                                                        FB[:, :].rearrange("p (g n) -> p g n", g=B), ALU.mult, ALU.add), "y1_read")
                    if rec:
                        store(l, 1, 0)
                        store(l, 1, 1)
                        if l >= 2:
                            add_off(l - 1, 1)
                        scale_ar(l, 1)
                        if l == 0:
                            start_inverse(1)
                    if l == 1 and front:
                        need(carried)
                        dve.wait_ge(S("xnc_done"), 1)
                        need(run(v.tensor_tensor(dx[:, :, :].rearrange("p c (g t) -> p (c g) t", g=B),
                                                 xnc[:, :, :, 0:L].rearrange("p c g t -> p (c g) t"),
                                                 xnc[:, :, :, 1:L + 1].rearrange("p c g t -> p (c g) t"), ALU.subtract)))
                        for c in range(2):
                            run(v.scalar_tensor_tensor(xm[:, c, :].rearrange("p (g t) -> p g t", g=B),
                                                       dx[:, c, :].rearrange("p (g t) -> p g t", g=B),
                                                       prm[:, P_XMIU + c:P_XMIU + c + 1], xnc[:, c, :, 1:L + 1],
                                                       ALU.mult, ALU.add), "xm_done")
                    if l == 3 and rec:
                        need(("y1_read", 1))
                        for g in range(B):
                            run(v.tensor_scalar(y1[:, g, :], y1[:, g, :], vsum[:, g:g + 1], None, ALU.mult), "ypre_done")
                    if l in (3, 4, 5) and front:
                        router(l - 3)
                    pieces(AFTER[l])
                    if l == 5 and front:
                        gate_sum()
                    if l == 5 and rec:
                        dve.wait_ge(S("ysg_done"), 1)
                        if post:
                            dve.wait_ge(S("o_read"), 1)
                        run(v.tensor_tensor(fgate[:, :, :], y1[:, :, :], ysg[:, :, :], ALU.mult), "fgate_done")
                    if l == 6 and front:
                        dve.wait_ge(S("sig_done"), 2)
                        if rec:
                            dve.wait_ge(S("tot_done"), 4)
                        run(v.tensor_scalar(tot[0][:, :, :, :], sig[:, :, :, :], math.exp(-0.5), None, ALU.mult), "d_done")
                if rec:
                    for g in range(B):
                        dve.wait_ge(S("x_mm"), 2 * (TOP - 1) + g + 1)
                        run(v.tensor_copy(xb[HALF:L, g, :, :], CB[g][HALF:L, 0:256].rearrange("p (h n) -> p h n", h=H)), "x_done")
                    for g in range(B):
                        dve.wait_ge(S("off_mm"), 2 * (TOP - 1) + g + 1)
                        run(v.tensor_copy(tinvT[0:HALF, g, :, HALF:L],
                                          CB[g][0:HALF, 256:512].rearrange("p (h n) -> p h n", h=H)), "inv_finished")
                if front:
                    dve.wait_ge(S("nrm_done"), 1)
                    need(run(v.tensor_scalar(nrm1[:, :, :], nrm[:, :, :], 1e-12, None, ALU.max)))
                    need(run(v.reciprocal(kinv[:, :, :], nrm1[:, :, :])))
                    dve.wait_ge(S("kraw_done"), 1)
                    need(run(v.tensor_tensor(kh[:, :, :, :], kraw[:, :, :, :],
                                             kinv[:, :, :].unsqueeze(2).to_broadcast([128, B, 2, L]), ALU.mult), "kh_done"))
                    dve.wait_ge(S("r_done"), 1)
                    for c in range(2):
                        run(v.scalar_tensor_tensor(dg[:, 2, :, c, :], rr[:, :, c, :], prm[:, P_XTIME + c:P_XTIME + c + 1],
                                                   kh[:, :, c, :], ALU.mult, ALU.mult), "dg2_done")
                    if rec:
                        dve.wait_ge(S("bkt_mm"), B)
                    dve.wait_ge(S("agate_done"), 2)
                    run(v.scalar_tensor_tensor(bk[:, :, 0, :, :].rearrange("p g c t -> p g (c t)"),
                                               kh[:, :, :, :].rearrange("p g c t -> p g (c t)"), 2.0,
                                               agate[:, :, :, :].rearrange("p g c t -> p g (c t)"), ALU.mult, ALU.mult),
                        "bk0_ready")
                if rec:
                    dve.wait_ge(S("tot_done"), 2 * LEVELS)
                    for g in range(B):
                        dve.wait_ge(S("inc_mm"), g + 1)
                        for c in range(2):
                            for o in (0, 64):
                                st = state[o:o + 64, g, c, o:o + 64]
                                run(v.scalar_tensor_tensor(st, st, tot[LEVELS][o:o + 64, g, c, :],
                                                           GB[g][o:o + 64, c * 128 + o:c * 128 + o + 64], ALU.mult, ALU.add))
                    dve.wait_ge(S("y_done"), B)
                    need(run(v.tensor_reduce(s8[:, :], yv, AX.X, ALU.add)))
                    need(run(v.tensor_scalar(mean8[:, :], s8[:, :], 1.0 / N, None, ALU.mult)))
                    run(v.tensor_tensor(yc[:, :, :], yv, mean8[:, :].unsqueeze(2).to_broadcast([128, B * H, N]),
                                        ALU.subtract), "yc_done")
                if front:
                    need(("d_done", 1))
                    run(v.tensor_tensor(ar[:, :, 1, :, :], rr[:, :, :, :], tot[0][:, :, :, :], ALU.mult), "ar1_ready")
                    hidden(0)
                    hidden(1)
                if rec:
                    dve.wait_ge(S("ysq_done"), 1)
                    run(v.tensor_reduce(v8[:, :], ysq[:, :, :], AX.X, ALU.add), "v8_done")
                    dve.wait_ge(S("sd8_done"), 1)
                    need(run(v.reciprocal(rs8[:, :], sd8[:, :])))
                    need(run(v.tensor_tensor(yn[:, :, :].rearrange("p g (h n) -> p (g h) n", n=N), yc[:, :, :],
                                             rs8[:, :].unsqueeze(2).to_broadcast([128, B * H, N]), ALU.mult)))
                    need(run(v.tensor_tensor(yn2[:, :, :], yn[:, :, :], w["gamma"][:].unsqueeze(1).to_broadcast([128, B, C]),
                                             ALU.mult)))
                    dve.wait_ge(S("bv_shifted"), 1)
                    need(run(v.tensor_tensor(yn[:, :, :], yn2[:, :, :], bv[:, :, :, :].rearrange("p g h n -> p g (h n)"),
                                             ALU.add)))
                    dve.wait_ge(S("gate_moved"), 1)
                    run(v.tensor_tensor(zz[:, :, :], yn[:, :, :], gate_r[:, :, :], ALU.mult), "zz_done")
                if not rec:
                    wait_loaded(dve, 2)
                    dve.wait_ge(zeroed_late, len(ZEROED_LATE))
                if front:
                    if rec:
                        dve.wait_ge(S("bv_done"), 1)
                    for g in range(B):
                        dve.wait_ge(S("diag_mm"), g + 1)
                        dgp = DIAG[g][:, 0:12].rearrange("p (j h) -> p j h", j=3)
                        for j in range(2):
                            run(v.copy_predicated(gm[:, g, :, j, :, 1, :],
                                                  mask_d[:].unsqueeze(1).unsqueeze(1).to_broadcast([128, 2, 2, L]),
                                                  dgp[:, j, :].rearrange("p (q c) -> p q c", q=2).unsqueeze(3)
                                                  .to_broadcast([128, 2, 2, L])), "diag_read")
                        run(v.tensor_copy(bonus[:, g, :].rearrange("p (c q) -> p c q", q=2),
                                          dgp[:, 2, :].rearrange("p (q c) -> p c q", q=2)), "diag_read")
                        hidden(2 + g)
                run(v.memset(scratch[:, 3:4], 0.0), "dve_end")

            v.memset(xnc[:], 0.0).then_inc(zeroed, 1)
            v.memset(eps[:, 0:1], EPS_LN).then_inc(zeroed, 1)
            v.memset(eps[:, 1:2], EPS_GN).then_inc(zeroed, 1)
            v.memset(scratch[:], 0.0).then_inc(zeroed, 1)
            dve.wait_ge(zeroed, NZ)
            wait_loaded(dve, 0)
            tile(1, True, False, False)
            with dve.Fori(0, TILES - 1) as i:
                tile(i + 2, True, True, True)
            tile(TILES + 1, False, True, True)
            tile(TILES + 2, False, False, True)

        @block.sync
        def _(sp):
            sp.dma_start(x_in[:, :, :], x[0]).then_inc(x_first, 16)
            sp.dma_start(prm[:], par).then_inc(loaded_by[0], 16)

            def load(i):
                for k in GROUPS[i]:
                    dst, src = (w[k], weights[k]) if k in w else (cst[k], consts[k])
                    sp.dma_start(dst[:], src).then_inc(loaded_by[i], 16)

            load(0)
            sp.wait_ge(x_first, 16)

            S("x_loaded"), S("out_stored")
            nums = [s.num for s in sems.values()]
            assert len(nums) == max(nums) - min(nums) + 1

            def tile(front, rec, post, x_next, out_now):
                sp.sem_inc(go, 1)
                if front and not rec:
                    load(1)
                    load(2)
                if front:
                    sp.wait_ge(S("xn_done"), B)
                    sp.wait_ge(S("xa_moved"), 1)
                    sp.dma_start(x_in[:, :, :], x_next).then_inc(S("x_loaded"), 16)
                if post:
                    sp.wait_ge(S("out_done"), 1)
                    sp.dma_start(out_now, out_t[:, :, :]).then_inc(S("out_stored"), 16)
                if front:
                    sp.wait_ge(S("down_mm"), 2)
                    sp.wait_ge(S("x_loaded"), 16)
                if rec:
                    sp.wait_ge(S("inc_mm"), B)
                if post:
                    sp.wait_ge(S("o_mm"), 1)
                    sp.wait_ge(S("out_stored"), 16)
                for e in ("act", "pool", "dve"):
                    sp.wait_ge(S(e + "_end"), 1)
                sp.sem_clear(range(min(nums), max(nums) + 1))

            tile(True, False, False, x[1], None)
            with sp.Fori(0, TILES - 1) as i:
                tile(True, True, True, x[i + 2], out[i])
            tile(False, True, True, None, out[TILES - 1])
            tile(False, False, True, None, out[TILES])


def kernel(**inputs):
    import numpy as np
    import concourse.bacc as bacc
    from concourse.bass_utils import run_bass_kernel_spmd as run_spmd

    a = {k[3:]: np.asarray(v) for k, v in inputs.items()}

    def halves(m):
        return np.ascontiguousarray(m.reshape(-1, 128, m.shape[-1]).transpose(1, 0, 2))

    def cols(v):
        return v.reshape(-1, 128).T

    par = np.zeros((128, P_COLS), np.float32)
    par[:, P_LAM:P_WMIU] = cols(a["attn_lambdas"])
    par[:, P_WMIU:P_ATIME] = cols(a["attn_w_miu"])
    par[:, P_ATIME:P_XMIU] = cols(a["attn_a_time"])
    par[:, P_XMIU:P_XTIME] = cols(a["attn_x_miu"])
    par[:, P_XTIME:P_BI] = cols(a["attn_x_time"])
    par[:, P_BI:P_COLS] = cols(a["ffn_bi"])
    x_b = np.zeros((128, 2, 256), np.float32)
    x_b[:, 0, :] = a["attn_x_B"][:4].reshape(128, 256)
    x_b[0:64, 1, :] = a["attn_x_B"][4:].reshape(64, 256)
    weights = {
        "x_A": halves(a["attn_x_A"]), "x_B": x_b,
        "w_A": halves(a["attn_w_A"]), "w_B": a["attn_w_B"], "k_A": halves(a["attn_k_A"]), "k_B": a["attn_k_B"],
        "a_A": halves(a["attn_a_A"]), "a_B": a["attn_a_B"], "g_A": halves(a["attn_g_A"]), "g_B": a["attn_g_B"],
        "rW": halves(a["attn_rW"].T), "kW": halves(a["attn_kW"].T), "vW": halves(a["attn_vW"].T), "oW": halves(a["attn_oW"].T),
        "route": halves(np.concatenate([a["ffn_lora_A"].reshape(128, 256).T, a["ffn_gate_w"].T], 1)),
        "wi": halves(a["ffn_wi"].T), "lora_B": a["ffn_lora_B"].transpose(0, 2, 1).reshape(128, 1024),
        "wo": halves(a["ffn_wo"].T),
        "gate_b": np.broadcast_to(a["ffn_gate_b"], (128, 8)), "bo": np.broadcast_to(a["ffn_bo"], (128, 256)),
        "gamma": np.broadcast_to(a["attn_gn_gamma"], (128, 256)), "beta": np.broadcast_to(a["attn_gn_beta"], (128, 256)),
    }
    tok = np.arange(128)
    mask_g = np.zeros((128, LEVELS, HALF), np.int32)
    mask_x = np.zeros((128, LEVELS, HALF), np.float32)
    for l in range(LEVELS):
        m = 1 << l
        lefts = tok[(tok // m) % 2 == 0]
        rights = tok[(tok // m) % 2 == 1]
        for j in range(HALF):
            mask_g[:, l, j] = (tok // (2 * m) == rights[j] // (2 * m)) & ((tok // m) % 2 == 0)
            mask_x[:, l, j] = (tok // (2 * m) == lefts[j] // (2 * m)) & ((tok // m) % 2 == 1)
    consts = {
        "ident": np.eye(128, dtype=np.float32), "ones": np.ones((128, 128), np.float32),
        "headsel": (tok[:, None] // 64 == np.arange(2)[None, :]).astype(np.float32),
        "mask_g": mask_g, "mask_x": mask_x, "mask_d": np.eye(128, dtype=np.int32),
        "rev8": np.broadcast_to(np.arange(8, 0, -1).astype(np.float32), (128, 8)),
    }
    xs = np.zeros((TILES + 1, L, B, C), np.float32)
    xs[:TILES] = a["attn_x"].reshape(B, TILES, L, C).transpose(1, 2, 0, 3)

    nc = bacc.Bacc("TRN2", target_bir_lowering=False, num_devices=1)
    arrays = {}

    def dram(name, arr):
        arrays[name] = np.ascontiguousarray(arr)
        return nc.dram_tensor(name, arr.shape, mybir.dt.from_np(arr.dtype), kind="ExternalInput").ap()

    x_ap, par_ap = dram("x", xs), dram("par", par)
    w_ap = {k: dram("w_" + k + "_dram", v) for k, v in weights.items()}
    c_ap = {k: dram("c_" + k + "_dram", v) for k, v in consts.items()}
    o_ap = nc.dram_tensor("out", (TILES + 1, L, B, C), F32, kind="ExternalOutput").ap()
    program(nc, x_ap, par_ap, w_ap, c_ap, o_ap)
    r = run_spmd(nc, [arrays], core_ids=[0])
    o = r.results[0]["out"][1:]
    return np.ascontiguousarray(o.reshape(TILES, L, B, C).transpose(2, 0, 1, 3).reshape(B, T, C))
```
